# Optimizing a Trainium2 kernel written in Bass

```python
import numpy as np
import jax
import jax.numpy as jnp

def _softmax(x, axis=-1):
    return jax.nn.softmax(x, axis=axis)

def _gelu(x):
    return jax.nn.gelu(x, approximate=True)

def _silu(x):
    return jax.nn.silu(x)

def _sigmoid(x):
    return jax.nn.sigmoid(x)

def _layernorm(x, axis=-1, eps=1e-05):
    m = jnp.mean(x, axis=axis, keepdims=True)
    v = jnp.var(x, axis=axis, keepdims=True)
    return (x - m) / jnp.sqrt(v + eps)

def _scatter_add(tgt, idx, src, axis=0):
    return tgt.at[idx].add(src)

def _segment_sum(src, seg, n):
    return jax.ops.segment_sum(src, seg, n)
kernel_name = 'mk_gnn_resnorm_d1_gnn_r8_82d4e1'

def setup_inputs(seed: int=0):
    np.random.seed(seed)
    _w = jnp.asarray

    def _rec_inputs():
        import jax
        import jax.numpy as jnp
        _gk = jax.random.key(seed)
        x = -0.000202 + 1 * jax.random.normal(jax.random.fold_in(_gk, 1), (12500, 128), jnp.float32)
        src = jax.random.randint(jax.random.fold_in(_gk, 2), (200000,), 0, 12500, jnp.int32)
        dst = jax.random.randint(jax.random.fold_in(_gk, 3), (200000,), 0, 12500, jnp.int32)
        _o = jnp.argsort(dst, stable=True)
        src = src[_o]
        dst = dst[_o]
        edge_attr_42 = 0.000171677 + 1.0001 * jax.random.normal(jax.random.fold_in(_gk, 11), (200000, 42), jnp.float32)
        edge_weight = jax.random.uniform(jax.random.fold_in(_gk, 13), (200000,), jnp.float32, 0.0, 0.999998)
        node_vec = jax.random.uniform(jax.random.fold_in(_gk, 14), (12500,), jnp.float32, 0.0, 0.999994)
        return (x, src, dst, edge_attr_42, edge_weight, node_vec)
    x, src, dst, edge_attr_42, edge_weight, node_vec = _rec_inputs()

    def _L0_gnn_setup():
        import jax, jax.numpy as jnp
        import numpy as np
        NODE_EMB_DIM = 16
        NUM_REL = 10

        def _rgcn_layer(x, src, dst, edge_type, w_rel, root, bias):
            N = x.shape[0]
            seg = dst * NUM_REL + edge_type
            xs = x[src]
            sums = jax.ops.segment_sum(xs, seg, num_segments=N * NUM_REL)
            cnt = jax.ops.segment_sum(jnp.ones(seg.shape, x.dtype), seg, num_segments=N * NUM_REL)
            mean = (sums / jnp.maximum(cnt, 1.0)[:, None]).reshape(N, NUM_REL, -1)
            return jnp.einsum('nrd,rdo->no', mean, w_rel) + x @ root + bias
        key = jax.random.key(seed)
        ks = jax.random.split(key, 10)
        N, E, C = (6250, 100000, 128)
        s = 1.0 / np.sqrt(C).astype(np.float32)
        x = jax.random.normal(ks[0], (N, C), jnp.float32)
        last_update = jax.random.uniform(ks[1], (N,), jnp.float32)
        t = jax.random.uniform(ks[2], (E,), jnp.float32)
        msg = jax.random.normal(ks[3], (E, 2 * NODE_EMB_DIM + NUM_REL), jnp.float32)
        w_rel1 = jax.random.normal(ks[4], (NUM_REL, C, C), jnp.float32) * s
        root1 = jax.random.normal(ks[5], (C, C), jnp.float32) * s
        b1 = jnp.zeros((C,), jnp.float32)
        w_rel2 = jax.random.normal(ks[6], (NUM_REL, C, C), jnp.float32) * s
        root2 = jax.random.normal(ks[7], (C, C), jnp.float32) * s
        b2 = jnp.zeros((C,), jnp.float32)
        edge_index = jax.random.randint(ks[8], (2, E), 0, N, dtype=jnp.int32)
        return dict(x=x, last_update=last_update, t=t, msg=msg, w_rel1=w_rel1, root1=root1, b1=b1, w_rel2=w_rel2, root2=root2, b2=b2, edge_index=edge_index)
    _L0_gnn_all = _L0_gnn_setup()
    _L0_gnn_in = {k: v for k, v in _L0_gnn_all.items() if k in ('w_rel1', 'root1', 'b1', 'w_rel2', 'root2', 'b2')}
    del _L0_gnn_all
    return {'x': x, 'src': src, 'dst': dst, 'edge_attr_42': edge_attr_42, 'edge_weight': edge_weight, 'node_vec': node_vec, 'L0_gnn_w_rel1': _L0_gnn_in['w_rel1'], 'L0_gnn_root1': _L0_gnn_in['root1'], 'L0_gnn_b1': _L0_gnn_in['b1'], 'L0_gnn_w_rel2': _L0_gnn_in['w_rel2'], 'L0_gnn_root2': _L0_gnn_in['root2'], 'L0_gnn_b2': _L0_gnn_in['b2']}

def reference(x, src, dst, edge_attr_42, edge_weight, node_vec, L0_gnn_w_rel1, L0_gnn_root1, L0_gnn_b1, L0_gnn_w_rel2, L0_gnn_root2, L0_gnn_b2):
    import jax
    import jax.numpy as jnp

    def _L0_gnn_ref(x, last_update, t, msg, w_rel1, root1, b1, w_rel2, root2, b2, edge_index):
        import jax, jax.numpy as jnp
        import numpy as np
        NODE_EMB_DIM = 16
        NUM_REL = 10

        def _rgcn_layer(x, src, dst, edge_type, w_rel, root, bias):
            N = x.shape[0]
            seg = dst * NUM_REL + edge_type
            xs = x[src]
            sums = jax.ops.segment_sum(xs, seg, num_segments=N * NUM_REL)
            cnt = jax.ops.segment_sum(jnp.ones(seg.shape, x.dtype), seg, num_segments=N * NUM_REL)
            mean = (sums / jnp.maximum(cnt, 1.0)[:, None]).reshape(N, NUM_REL, -1)
            return jnp.einsum('nrd,rdo->no', mean, w_rel) + x @ root + bias
        src, dst = (edge_index[0], edge_index[1])
        edge_type = jnp.argmax(msg[:, NODE_EMB_DIM:-NODE_EMB_DIM], axis=1).astype(jnp.int32)
        h = jax.nn.relu(_rgcn_layer(x, src, dst, edge_type, w_rel1, root1, b1))
        return _rgcn_layer(h, src, dst, edge_type, w_rel2, root2, b2)
    edge_index = jnp.stack([src, dst])
    x = _layernorm(x + _L0_gnn_ref(x, node_vec, edge_weight, edge_attr_42, L0_gnn_w_rel1, L0_gnn_root1, L0_gnn_b1, L0_gnn_w_rel2, L0_gnn_root2, L0_gnn_b2, edge_index), axis=-1)
    return x

_drawn_inputs = setup_inputs


def setup_inputs(seed=0):
    import zlib

    import numpy as np

    out = dict(_drawn_inputs(seed))
    spreads = {'L0_gnn_b1': (0.0, 0.1), 'L0_gnn_b2': (0.0, 0.386)}
    factors = {}
    for name, (base, spread) in spreads.items():
        noise = np.random.default_rng([zlib.crc32(name.encode()), seed]).standard_normal(out[name].shape)
        drawn = base * np.exp(spread * noise) if base else spread * noise
        out[name] = jnp.asarray(drawn.astype(out[name].dtype))
    for name, factor in factors.items():
        out[name] = (out[name] * factor).astype(out[name].dtype)
    return out
```

```python
import concourse.bass as bass
from concourse import mybir
from contextlib import ExitStack


F32 = mybir.dt.float32
BF16 = mybir.dt.bfloat16
I32 = mybir.dt.int32
U32 = mybir.dt.uint32
ALU = mybir.AluOpType
ACT = mybir.ActivationFunctionType
AX = mybir.AxisListType

N = 12500
E = 200000
C = 128
R = 10
MSG = 42
TYPE0 = 16
P = 128
GT = 8
GE = GT * P
NGROUP = -(-E // GE)
GPAD = 4
NG = NGROUP + GPAD
W = 96
U = 4
TURNS = NGROUP // U
FARW = 512
NFAR = -(-N // FARW)
NCOL = NFAR * FARW
SPARE = N + 100
NBLOCK = -(-N // P)
NPAIR = NBLOCK // 2
LASTN = N - (NBLOCK - 1) * P
RC = R * C
YCHUNK = [(0, 512), (512, 512), (1024, 256)]
LAG = 2
PADDST = 1.0e6
CH = 32
NCH = GE // CH
HALF = [(0, P), (P, NGROUP - P)]
LASTE = E - (NGROUP - 1) * GE
LASTCH = LASTE // CH
EPS = 1e-5
assert TURNS * U == NGROUP and NPAIR * 2 == NBLOCK and LASTCH * CH == LASTE
assert TURNS == NPAIR and SPARE + W <= NCOL


def gnn_kernel(nc, x, src, dst, edge_attr, w_rel1, root1, b1, w_rel2, root2, b2, out, table1, table2,
               type_row, row_scratch):
    ctx = ExitStack()
    with ctx:
        def sb(name, shape, dt=F32):
            return ctx.enter_context(nc.sbuf_tensor(name, shape, dt))

        def sem(name):
            return ctx.enter_context(nc.semaphore(name))

        ident = sb("ident", [P, P])
        iota_w = sb("iota_w", [P, W])
        iota_far = sb("iota_far", [P, FARW])
        iota_r = sb("iota_r", [P, R])
        rev_r = sb("rev_r", [P, R])
        part = sb("part", [P, 1])
        far0 = sb("far0", [P, NFAR])
        turn_min = sb("turn_min", [1, TURNS])
        eps = sb("eps", [P, 1])
        wall = [sb(f"wall{l}", [P, R, C]) for l in range(2)]
        root = [sb(f"root{l}", [P, C]) for l in range(2)]
        bias = [sb(f"bias{l}", [P, 1]) for l in range(2)]
        rel_t = sb("rel_t", [P, NG * GT])
        typ_t = sb("typ_t", [P, NG * GT])
        far_t = sb("far_t", [P, NG * GT])
        idx_t = sb("idx_t", [P, NG * GT], U32)
        c_t = sb("c_t", [P, NG * GT])
        acc = sb("acc", [P, NCOL])
        cnt = sb("cnt", [P, NCOL])
        dst_i = [cnt[:, h * GE:(h + 1) * GE].bitcast(I32) for h in range(2)]
        src_i = [cnt[:, (2 + h) * GE:(3 + h) * GE].bitcast(I32) for h in range(2)]
        typ_g = [cnt[:, (4 + h) * GE:(5 + h) * GE] for h in range(2)]
        rel_g = [cnt[:, (6 + h) * GE:(7 + h) * GE] for h in range(2)]
        far_g = [cnt[:, (8 + h) * GE:(9 + h) * GE] for h in range(2)]
        idx_g = [cnt[:, (10 + h) * GE:(11 + h) * GE] for h in range(2)]
        attr = sb("attr", [P, 2, CH, MSG])
        amax = sb("amax", [P, 2, CH])
        ahit = sb("ahit", [P, CH, R])
        gmin = sb("gmin", [P, 2])
        gmax = sb("gmax", [P, 2])
        row_min = sb("row_min", [1, NG])
        row_max = sb("row_max", [1, NG])
        row_base = sb("row_base", [1, NG], I32)
        row_count = sb("row_count", [1, NG], I32)
        row_tmp = sb("row_tmp", [1, NG])
        flag = sb("flag", [1, 8])
        flag_i = sb("flag_i", [1, 2], I32)
        x_in = sb("x_in", [P, 2, C])
        h_s = sb("h_s", [P, 2, P])
        y_out = sb("y_out", [P, 2, RC])
        rows = sb("rows", [P, U, GT, C])
        idx_s = sb("idx_s", [P, U, GT], U32)
        hit = sb("hit", [P, U, GT, W], BF16)
        hit_typ = sb("hit_typ", [P, U, GT, R], BF16)
        typ_oh = sb("typ_oh", [R, 2, GE])
        cnt_e = sb("cnt_e", [P, GT])
        z = y_out[:, 0, 0:2 * C].rearrange("p (q c) -> p q c", q=2)
        zo = y_out[:, 1, 0:2 * C].rearrange("p (q c) -> p q c", q=2)
        stats = sb("stats", [P, 2, 6])
        mv = sb("mv", [P, 2, 2])
        std = sb("std", [P, 2])
        rstd = sb("rstd", [P, 2])
        room = attr[:, :, :, :].rearrange("p a b c -> p (a b c)")
        S = room[:, 0:2 * GT * W].rearrange("p (q j w) -> p q j w", q=2, j=GT)
        looked = room[:, 2 * GT * W:3 * GT * W].rearrange("p (j w) -> p j w", j=GT)
        far_hit = room[:, 0:FARW]
        far_hitb = room[:, FARW:FARW + FARW // 2].bitcast(BF16)
        far_d = sb("far_d", [P, NFAR])
        far_c = sb("far_c", [P, NFAR])

        ps_look = ctx.enter_context(nc.psum_tensor("ps_look", [P, 2, 512], F32))
        ps_agg = ctx.enter_context(nc.psum_tensor("ps_agg", [P, 512], F32))
        ps_cnt = ctx.enter_context(nc.psum_tensor("ps_cnt", [P, 512], F32))
        ps_y = [ctx.enter_context(nc.psum_tensor(f"ps_y{k}", [P, 512], F32)) for k in range(3)]
        ps_root = ctx.enter_context(nc.psum_tensor("ps_root", [P, 512], F32))

        sums = ps_agg[:, 0:W]
        counts = ps_cnt[0:R, 0:W]
        ps_xt = [ps_cnt, ps_agg]
        ps_fin = ps_cnt[:, 0:2 * P].rearrange("p (q n) -> p q n", q=2)

        consts_done = sem("consts_done")
        weights_in = sem("weights_in")
        edges_in = sem("edges_in")
        pad_set = sem("pad_set")
        attr_in = [sem(f"attr_in{q}") for q in range(2)]
        attr_used = sem("attr_used")
        grouped = sem("grouped")
        type_saved = sem("type_saved")
        minmax_saved = sem("minmax_saved")
        minmax_in = sem("minmax_in")
        tr_ready = sem("tr_ready")
        tr_taken = sem("tr_taken")
        flags_done = sem("flags_done")
        tables_done = sem("tables_done")
        x_loaded = [sem(f"x_loaded{q}") for q in range(2)]
        xt_ready = sem("xt_ready")
        xt_done = sem("xt_done")
        y_ready = sem("y_ready")
        y_taken = sem("y_taken")
        root_ready = sem("root_ready")
        root_done = sem("root_done")
        relu_done = sem("relu_done")
        y_stored = [sem(f"y_stored{q}") for q in range(2)]
        idx_ready = sem("idx_ready")
        rows_in = [sem(f"rows_in{s}") for s in range(U)]
        typ_in = [sem(f"typ_in{q}") for q in range(2)]
        oh_ready = sem("oh_ready")
        look_ready = sem("look_ready")
        look_taken = sem("look_taken")
        hit_ready = sem("hit_ready")
        cnt_ready = sem("cnt_ready")
        cnt_done = sem("cnt_done")
        S_ready = sem("S_ready")
        agg_ready = sem("agg_ready")
        agg_done = sem("agg_done")
        own = sem("own")
        held = sem("held")
        own_loop = [sem(f"own_loop{k}") for k in range(8)]
        pre_hit = sem("pre_hit")
        pre_ready = sem("pre_ready")
        pre_done = sem("pre_done")
        fin_x = sem("fin_x")
        fin_copied = sem("fin_copied")
        fin_ready = sem("fin_ready")
        fin_z = sem("fin_z")
        fin_std = sem("fin_std")
        fin_out = sem("fin_out")
        fin_saved = sem("fin_saved")
        far_a = [sem(f"far_a{k}") for k in range(4)]
        far_b = [sem(f"far_b{k}") for k in range(4)]
        far_v = [sem(f"far_v{k}") for k in range(4)]
        far_idx = [sem(f"far_idx{k}") for k in range(2)]
        far_rows = [sem(f"far_rows{k}") for k in range(2)]
        far_ask = sem("far_ask")
        far_typ = sem("far_typ")
        far_end = sem("far_end")

        tables = [table1, table2]
        NCONST = 10

        def tiles(tab, g, n=1):
            return tab[:, bass.ds(g * GT, n * GT)]

        SPANS = [(0, LAG, False), (LAG, TURNS, True)]

        blk = ctx.enter_context(nc.Block())

        @blk.gpsimd
        def _(pool):
            g_ = nc.gpsimd
            g_.memset(ident[:], 0.0).then_inc(consts_done, 1)
            pool.wait_ge(consts_done, 1)
            g_.affine_select(out=ident[:], in_=ident[:], compare_op=ALU.not_equal, fill=1.0, base=0,
                             pattern=[[-1, P]], channel_multiplier=1).then_inc(consts_done, 1)
            for tile, step, base, mult in ((iota_w, 1, 0, 0), (iota_far, 1, 0, 0), (iota_r, 1, 0, 0),
                                           (rev_r, -1, R, 0), (part, 0, 0, 1), (far0, FARW, 0, 0)):
                g_.iota(tile[:], pattern=[[step, tile.shape[1]]], base=base, channel_multiplier=mult,
                        allow_small_or_imprecise_dtypes=True).then_inc(consts_done, 1)
            g_.iota(turn_min[:], pattern=[[U * P // 2, TURNS]], base=-(LAG - 1) * U * P // 2,
                    channel_multiplier=0, allow_small_or_imprecise_dtypes=True).then_inc(consts_done, 1)
            g_.memset(eps[:], EPS).then_inc(consts_done, 1)

            pool.wait_ge(pad_set, 3)
            for h, (g0, ng) in enumerate(HALF):
                full = ng if h == 0 else 64
                for ap, tile in ((dst, dst_i[h]), (src, src_i[h])):
                    pool.dma_start(tile[0:full, :], ap[g0 * GE:(g0 + full) * GE].rearrange("(g k) -> g k", k=GE)
                                   ).then_inc(edges_in, 16)
                    if full < ng:
                        pool.dma_start(tile[full:ng - 1, :], ap[(g0 + full) * GE:(g0 + ng - 1) * GE]
                                       .rearrange("(g k) -> g k", k=GE)).then_inc(edges_in, 16)
                        pool.dma_start(tile[ng - 1:ng, 0:LASTE], ap[E - LASTE:E].rearrange("(g k) -> g k", g=1)
                                       ).then_inc(edges_in, 16)

            def load_attr(h, q, ch, used, with_last):
                g0, ng = HALF[h]
                pool.wait_ge(attr_used, used)
                full = ng if h == 0 else 64
                parts = [(0, full)] if h == 0 else [(0, full), (full, ng - 1)]
                for a, b in parts:
                    view = edge_attr[(g0 + a) * GE:(g0 + b) * GE, :].rearrange("(g k) m -> g k m", k=GE)
                    pool.dma_start(attr[a:b, q, :, :], view[:, bass.ds(ch * CH, CH), :]).then_inc(attr_in[q], 16)
                if h == 1:
                    if with_last:
                        view = edge_attr[E - LASTE:E, :].rearrange("(g k) m -> g k m", g=1)
                        pool.dma_start(attr[ng - 1:ng, q, :, :], view[:, bass.ds(ch * CH, CH), :]
                                       ).then_inc(attr_in[q], 16)

            with pool.Fori(0, NCH // 2) as i:
                for q in range(2):
                    load_attr(0, q, i * 2 + q, i * 2 + q + 1, False)
            with pool.Fori(0, LASTCH // 2) as i:
                for q in range(2):
                    load_attr(1, q, i * 2 + q, i * 2 + (NCH + q + 1), True)
            with pool.Fori(LASTCH // 2, NCH // 2) as i:
                for q in range(2):
                    load_attr(1, q, i * 2 + q, i * 2 + (NCH + q + 1), False)

            for l in range(2):
                for q in range(2):
                    pool.wait_ge(y_stored[q], 16 * NPAIR * (l + 1))
                with pool.Fori(0, TURNS) as i:
                    for s in range(U):
                        pool.wait_ge(idx_ready, i * U + (l * NG + s + 1))
                        pool.sem_inc(held, 1)
                        for j in range(GT):
                            pool.indirect_dma_start(
                                out=rows[:, s, j, :], out_offset=None, in_=tables[l][:, :],
                                in_offset=bass.IndirectOffsetOnAxis(ap=idx_s[:, s, j:j + 1], axis=0)
                            ).then_inc(rows_in[s], 16)
                far = pool.value_load(flag_i[0:1, 1:2], min_val=0, max_val=1)
                with pool.If(far > 0):
                    with pool.Fori(0, NGROUP * GT) as t:
                        pool.wait_ge(far_idx[l], t + 1)
                        pool.sem_inc(held, 1)
                        pool.indirect_dma_start(
                            out=rows[:, 0, 0, :], out_offset=None, in_=tables[l][:, :],
                            in_offset=bass.IndirectOffsetOnAxis(ap=idx_s[:, 0, 0:1], axis=0)
                        ).then_inc(far_rows[l], 16)

        @blk.sync
        def _(sp):
            for l, (w, r, b) in enumerate(((w_rel1, root1, b1), (w_rel2, root2, b2))):
                sp.dma_start(wall[l][:, :, :], w.rearrange("r d o -> d r o")).then_inc(weights_in, 16)
                sp.dma_start(root[l][:, :], r[:, :]).then_inc(weights_in, 16)
                sp.dma_start(bias[l][:, :], b.rearrange("(o u) -> o u", u=1)).then_inc(weights_in, 16)

            def load_x(b, q, n, freed):
                if freed is not None:
                    sp.wait_ge(xt_ready, freed)
                sp.dma_start(x_in[0:n, q, :], x[bass.ds(b * P, n), :]).then_inc(x_loaded[q], 16)

            load_x(0, 0, P, None)
            load_x(1, 1, P, None)
            with sp.Fori(1, NPAIR - 1) as u:
                for q in range(2):
                    load_x(u * 2 + q, q, P, u * 2 + (q - 1))
            load_x(NBLOCK - 2, 0, P, NBLOCK - 3)
            load_x(NBLOCK - 1, 1, LASTN, NBLOCK - 2)

            for h, (g0, ng) in enumerate(HALF):
                sp.wait_ge(grouped, h + 1)
                sp.dma_start(type_row[g0:g0 + ng, :], typ_g[h][0:ng, :]).then_inc(type_saved, 16)
                for k, col in enumerate((gmin, gmax)):
                    sp.dma_start(row_scratch[k:k + 1, g0:g0 + ng].rearrange("k g -> g k"), col[0:ng, h:h + 1]
                                 ).then_inc(minmax_saved, 16)
            sp.wait_ge(minmax_saved, 64)
            sp.dma_start(row_min[0:1, 0:NGROUP], row_scratch[0:1, 0:NGROUP]).then_inc(minmax_in, 16)
            sp.dma_start(row_max[0:1, 0:NGROUP], row_scratch[1:2, 0:NGROUP]).then_inc(minmax_in, 16)

            def load_types(g, q, freed):
                if freed is not None:
                    sp.wait_ge(look_ready, freed)
                sp.dma_start(typ_oh[:, q, :], type_row[bass.ds(g, 1), :].to_broadcast([R, GE])
                             ).then_inc(typ_in[q], 16)

            sp.wait_ge(type_saved, 32)
            load_types(0, 0, None)
            load_types(1, 1, None)
            with sp.Fori(0, TURNS - 1) as i:
                for s in range(U):
                    load_types(i * U + (s + 2), s % 2, i * U + (s + 1))
            for s in range(U - 2):
                load_types((TURNS - 1) * U + s + 2, s % 2, (TURNS - 1) * U + s + 1)
            sp.wait_ge(flags_done, 1)
            far = sp.value_load(flag_i[0:1, 1:2], min_val=0, max_val=1)
            with sp.If(far > 0):
                flat = type_row.rearrange("g k -> (g k)")
                with sp.Fori(0, NGROUP * GT) as t:
                    sp.wait_ge(far_ask, t + 1)
                    sp.dma_start(typ_oh[:, 0, 0:P],
                                 flat[bass.ds(t * P, P)].rearrange("(u k) -> u k", u=1).to_broadcast([R, P])
                                 ).then_inc(far_typ, 16)

            def fin_io(u, last, first):
                if not first:
                    sp.wait_ge(fin_z, u + 1)
                    sp.sem_inc(held, 1)
                    sp.wait_ge(fin_saved, u * 16)
                    sp.sem_inc(held, 1)
                if last:
                    sp.dma_start(x_in[:, 0, :], x[(NBLOCK - 2) * P:(NBLOCK - 1) * P, :]).then_inc(fin_x, 16)
                    sp.dma_start(x_in[0:LASTN, 1, :], x[(NBLOCK - 1) * P:N, :]).then_inc(fin_x, 16)
                else:
                    sp.dma_start(x_in[:, :, :], x[bass.ds(u * (2 * P), 2 * P), :]
                                 .rearrange("(q p) c -> p q c", q=2)).then_inc(fin_x, 16)
                sp.wait_ge(fin_out, u + 2)
                if last:
                    sp.dma_start(out[(NBLOCK - 2) * P:(NBLOCK - 1) * P, :], zo[:, 0, :]).then_inc(fin_saved, 16)
                    sp.dma_start(out[(NBLOCK - 1) * P:N, :], zo[0:LASTN, 1, :]).then_inc(fin_saved, 16)
                else:
                    sp.dma_start(out[bass.ds(u * (2 * P), 2 * P), :].rearrange("(q p) c -> p q c", q=2),
                                 zo[:, :, :]).then_inc(fin_saved, 16)

            for q in range(2):
                sp.wait_ge(y_stored[q], 16 * NPAIR * 2)
            fin_io(0, False, True)
            with sp.Fori(1, NPAIR - 1) as u:
                fin_io(u, False, False)
            fin_io(NPAIR - 1, True, False)
            sp.wait_ge(fin_saved, 16 * (NPAIR + 1))

        @blk.scalar
        def _(act):
            a_ = nc.scalar

            def take_xt(b, q, n, used):
                act.wait_ge(xt_ready, b + 1)
                if used is not None:
                    act.wait_ge(root_ready, used)
                a_.copy(h_s[:, q, 0:n], ps_xt[q][:, 0:n]).then_inc(xt_done, 1)

            def take_block(l, u, q, n, first=False):
                b = u * 2 + q
                bt = b + l * NBLOCK
                for k, (o, w) in enumerate(YCHUNK):
                    act.wait_ge(y_ready, bt * 3 + (k + 1))
                    if k == 0 and not first:
                        act.wait_ge(y_stored[q], (u + l * NPAIR) * 16)
                    a_.copy(y_out[0:n, q, o:o + w], ps_y[k][0:n, 0:w]).then_inc(y_taken, 1)
                act.wait_ge(root_ready, bt + 1)
                a_.activation(acc[:, bass.ds(b * P, n)], ps_root[:, 0:n], ACT.Identity,
                              bias=bias[l][:, 0:1]).then_inc(root_done, 1)
                act.wait_ge(y_taken, bt * 3 + 6)
                rows_v = tables[l].rearrange("(m r) c -> m (r c)", r=R)
                act.dma_start(rows_v[bass.ds(b * P, n), :], y_out[0:n, q, :]).then_inc(y_stored[q], 16)

            act.wait_ge(weights_in, 16 * 6)
            take_xt(0, 0, P, None)
            take_xt(1, 1, P, None)
            for q in range(2):
                take_block(0, 0, q, P, first=True)
                take_xt(2 + q, q, P, q + 1)
            with act.Fori(1, NPAIR - 2) as u:
                for q in range(2):
                    take_block(0, u, q, P)
                    take_xt(u * 2 + (2 + q), q, P, u * 2 + (q + 1))
            for q in range(2):
                take_block(0, NPAIR - 2, q, P)
                take_xt(NBLOCK - 2 + q, q, LASTN if q else P, NBLOCK - 3 + q)
            for q in range(2):
                take_block(0, NPAIR - 1, q, LASTN if q else P)

            act.wait_ge(tables_done, 1)
            stream = act.value_load(flag_i[0:1, 0:1], min_val=0, max_val=1)
            far = act.value_load(flag_i[0:1, 1:2], min_val=0, max_val=1)

            def give_indices(g, s):
                a_.copy(idx_s[:, s, :], tiles(idx_t, g)).then_inc(idx_ready, 1)

            def next_indices(l, i, s):
                act.wait_ge(agg_ready, i * U + (l * NGROUP + s + 1))
                give_indices(i * U + (U + s), s)

            def relu(u, last=False):
                n = P + LASTN if last else 2 * P
                a_.activation(h_s[:, :, :].rearrange("p q n -> p (q n)")[:, 0:n], acc[:, bass.ds(u * (2 * P), n)],
                              ACT.Relu).then_inc(relu_done, 1)

            def pair(u, last=False):
                relu(u, last)
                for q in range(2):
                    take_block(1, u, q, LASTN if (last and q) else P)

            for s in range(U):
                give_indices(s, s)
            for start, end, behind in SPANS:
                with act.Fori(start, end) as i:
                    for s in range(U):
                        next_indices(0, i, s)
                        if behind and s in (0, 2):
                            with act.If(stream > 0):
                                if s == 0:
                                    act.wait_ge(agg_done, i * U + 1)
                                    relu(i - LAG)
                                take_block(1, i - LAG, s // 2, P)
            act.wait_ge(agg_done, NGROUP + 1)
            with act.If(far > 0):
                act.wait_ge(far_end, 1)
            with act.If(stream < 1):
                with act.Fori(0, TURNS - LAG) as u:
                    pair(u)
            pair(NPAIR - 2)
            pair(NPAIR - 1, last=True)

            def copy_pair(u, last=False):
                n = P + LASTN if last else 2 * P
                act.wait_ge(fin_ready, u + 1)
                a_.copy(h_s[:, :, :].rearrange("p q n -> p (q n)")[:, 0:n], acc[:, bass.ds(u * (2 * P), n)]
                        ).then_inc(fin_copied, 1)

            def root_of_variance(u):
                act.wait_ge(fin_z, u + 2)
                a_.activation(std[:, :], mv[:, :, 1], ACT.Sqrt, bias=eps[:, 0:1]).then_inc(fin_std, 1)

            for s in range(U):
                give_indices(s, s)
            for start, end, behind in SPANS:
                with act.Fori(start, end) as i:
                    for s in range(U):
                        next_indices(1, i, s)
                        if behind and s < 2:
                            with act.If(stream > 0):
                                if s == 0:
                                    act.wait_ge(agg_done, i * U + (NGROUP + 1))
                                    copy_pair(i - LAG)
                                else:
                                    root_of_variance(i - LAG)
            act.wait_ge(agg_done, 2 * NGROUP + 1)
            with act.If(far > 0):
                act.wait_ge(far_end, 2)
            with act.If(stream < 1):
                with act.Fori(0, TURNS - LAG) as u:
                    copy_pair(u)
                    root_of_variance(u)
            copy_pair(NPAIR - 2)
            root_of_variance(NPAIR - 2)
            copy_pair(NPAIR - 1, last=True)
            root_of_variance(NPAIR - 1)

        @blk.tensor
        def _(pe):
            t_ = nc.tensor

            def turn_x(b, q, n, taken):
                pe.wait_ge(x_loaded[q], taken[0])
                if taken[1] is not None:
                    pe.wait_ge(xt_done, taken[1])
                t_.transpose(ps_xt[q][:, 0:n], x_in[0:n, q, :], ident[0:n, 0:n]).then_inc(xt_ready, 1)

            def make_block(l, u, q, n, mid=None):
                b = u * 2 + q
                bt = b + l * NBLOCK
                h = h_s[:, q, 0:n]
                w = wall[l][:, :, :].rearrange("d r o -> d (r o)")
                for k, (o, wid) in enumerate(YCHUNK):
                    pe.wait_ge(y_taken, bt * 3 + (k + 1))
                    t_.matmul(ps_y[k][0:n, 0:wid], lhsT=h, rhs=w[:, o:o + wid], start=True, stop=True
                              ).then_inc(y_ready, 1)
                pe.wait_ge(root_done, bt + 1)
                t_.matmul(ps_root[:, 0:n], lhsT=root[l][:, :], rhs=h, start=True, stop=True
                          ).then_inc(root_ready, 1)

            pe.wait_ge(consts_done, NCONST)
            pe.wait_ge(weights_in, 16 * 6)
            turn_x(0, 0, P, (16, None))
            turn_x(1, 1, P, (16, None))
            with pe.Fori(0, NPAIR - 2) as u:
                for q in range(2):
                    pe.wait_ge(xt_done, u * 2 + (q + 1))
                    make_block(0, u, q, P)
                    turn_x(u * 2 + (2 + q), q, P, (u * 16 + 32, u * 2 + (q + 1)))
            for q in range(2):
                pe.wait_ge(xt_done, NBLOCK - 3 + q)
                make_block(0, NPAIR - 2, q, P)
                turn_x(NBLOCK - 2 + q, q, LASTN if q else P, (16 * NPAIR, NBLOCK - 3 + q))
            for q in range(2):
                pe.wait_ge(xt_done, NBLOCK - 1 + q)
                make_block(0, NPAIR - 1, q, LASTN if q else P)

            k = 0
            for h, (g0, ng) in enumerate(HALF):
                pe.wait_ge(grouped, h + 1)
                for tab in (rel_g, typ_g, far_g, idx_g):
                    for half in range(2):
                        if k >= 2:
                            pe.wait_ge(tr_taken, k - 1)
                        for j in range(4):
                            e0 = (half * 4 + j) * P
                            last = t_.transpose(ps_look[:, k % 2, j * P:j * P + ng], tab[h][0:ng, e0:e0 + P],
                                                ident[0:ng, 0:ng])
                        last.then_inc(tr_ready, 1)
                        k += 1

            pe.wait_ge(flags_done, 1)
            stream = pe.value_load(flag_i[0:1, 0:1], min_val=0, max_val=1)
            far = pe.value_load(flag_i[0:1, 1:2], min_val=0, max_val=1)

            def count(slot):
                for j in range(GT):
                    last = t_.matmul(counts, lhsT=hit_typ[:, slot, j, :], rhs=hit[:, slot, j, :],
                                     start=(j == 0), stop=(j == GT - 1))
                return last

            with pe.If(stream < 1):
                with pe.Fori(0, NGROUP) as g:
                    pe.wait_ge(pre_hit, g + 1)
                    count(0).then_inc(pre_ready, 1)
                with pe.If(far > 0):
                    with pe.Fori(0, NGROUP * GT) as t:
                        with pe.Fori(0, NFAR) as k:
                            pe.wait_ge(far_a[0], t * NFAR + k + 1)
                            t_.matmul(ps_y[0][0:R, :], lhsT=hit_typ[:, 0, 0, :], rhs=far_hitb, start=True,
                                      stop=True).then_inc(far_b[0], 1)

            for g in range(U):
                pe.wait_ge(hit_ready, g + 1)
                if g:
                    pe.wait_ge(cnt_done, g)
                count(g).then_inc(cnt_ready, 1)

            def aggregate(l, i, s):
                pe.wait_ge(S_ready, i * U + (l * NGROUP + s + 1))
                pe.wait_ge(rows_in[s], i * (16 * GT) + (16 * GT * (l * TURNS + 1)))
                pe.wait_ge(agg_done, i * U + (l * NGROUP + s + 1))
                for j in range(GT):
                    last = t_.matmul(sums, lhsT=rows[:, s, j, :], rhs=S[:, s % 2, j, :],
                                     start=(j == 0), stop=(j == GT - 1))
                last.then_inc(agg_ready, 1)

            for start, end, behind in SPANS:
                with pe.Fori(start, end) as i:
                    for s in range(U):
                        g = i * U + s
                        base = pe.value_load(row_base[0:1, bass.ds(g, 1)], min_val=0, max_val=N - 1)
                        pe.wait_ge(oh_ready, g + 1)
                        pe.wait_ge(look_taken, g + 1)
                        pe.wait_ge(cnt_done, g + 3)
                        for j in range(GT):
                            last = t_.matmul(ps_look[:, j // 4, (j % 4) * W:(j % 4 + 1) * W],
                                             lhsT=typ_oh[:, s % 2, j * P:(j + 1) * P],
                                             rhs=cnt[0:R, bass.ds(base, W)], start=True, stop=True)
                        last.then_inc(look_ready, 1)
                        aggregate(0, i, s)
                        pe.wait_ge(hit_ready, g + (U + 1))
                        pe.wait_ge(cnt_done, g + U)
                        count(s).then_inc(cnt_ready, 1)
                        if behind and s in (0, 2):
                            with pe.If(stream > 0):
                                if s == 0:
                                    pe.wait_ge(relu_done, i - (LAG - 1))
                                make_block(1, i - LAG, s // 2, P)
            with pe.If(far > 0):
                with pe.Fori(0, NGROUP * GT) as t:
                    with pe.Fori(0, NFAR) as k:
                        pe.wait_ge(far_a[1], t * NFAR + k + 1)
                        t_.matmul(ps_y[0][:, :], lhsT=typ_oh[:, 0, 0:P], rhs=cnt[0:R, bass.ds(k * FARW, FARW)],
                                  start=True, stop=True).then_inc(far_b[1], 1)

            def far_sums(l):
                with pe.Fori(0, NGROUP * GT) as t:
                    with pe.Fori(0, NFAR) as k:
                        pe.wait_ge(far_rows[l], t * 16 + 16)
                        pe.wait_ge(far_a[2 + l], t * NFAR + k + 1)
                        t_.matmul(ps_y[0][:, :], lhsT=rows[:, 0, 0, :], rhs=far_hit, start=True,
                                  stop=True).then_inc(far_b[2 + l], 1)

            with pe.If(far > 0):
                far_sums(0)
            with pe.If(stream < 1):
                with pe.Fori(0, TURNS - LAG) as u:
                    pe.wait_ge(relu_done, u + 1)
                    for q in range(2):
                        make_block(1, u, q, P)
            for u in (NPAIR - 2, NPAIR - 1):
                pe.wait_ge(relu_done, u + 1)
                for q in range(2):
                    make_block(1, u, q, LASTN if (u == NPAIR - 1 and q) else P)

            def turn_pair(u, last=False):
                pe.wait_ge(fin_z, u + 1)
                pe.wait_ge(fin_copied, u + 1)
                for q in range(2):
                    n = LASTN if (last and q) else P
                    ins = t_.transpose(ps_fin[0:n, q, :], h_s[:, q, 0:n], ident[:, :])
                ins.then_inc(fin_ready, 1)

            for start, end, behind in SPANS:
                with pe.Fori(start, end) as i:
                    for s in range(U):
                        aggregate(1, i, s)
                        if behind and s == 0:
                            with pe.If(stream > 0):
                                turn_pair(i - LAG)
            with pe.If(far > 0):
                far_sums(1)
            with pe.If(stream < 1):
                with pe.Fori(0, TURNS - LAG) as u:
                    turn_pair(u)
            turn_pair(NPAIR - 2)
            turn_pair(NPAIR - 1, last=True)

        @blk.vector
        def _(dve):
            v_ = nc.vector
            steps = [0]

            def link(ins):
                steps[0] += 1
                ins.then_inc(own, 1)
                dve.wait_ge(own, steps[0])

            def link_in(k, i, per, n, ins):
                ins.then_inc(own_loop[k], 1)
                dve.wait_ge(own_loop[k], i * per + (n + 1))

            dve.sem_inc(y_taken, 3)
            dve.sem_inc(root_done, 1)
            dve.sem_inc(look_taken, 1)
            dve.sem_inc(agg_done, 1)
            dve.sem_inc(attr_used, 2)
            for credited in (pre_done, fin_ready, fin_z, fin_out, *far_v):
                dve.sem_inc(credited, 1)

            v_.memset(dst_i[1][64:HALF[1][1], :], int(PADDST)).then_inc(pad_set, 1)
            v_.memset(src_i[1][64:HALF[1][1], :], 0).then_inc(pad_set, 1)
            v_.memset(acc[:, N:NCOL], 0.0).then_inc(pad_set, 1)
            link(v_.memset(row_min[:, :], float(N)))
            link(v_.memset(row_max[:, :], float(N)))
            npt = GPAD * GT
            link(v_.memset(rel_t[:, NGROUP * GT:NG * GT], PADDST))
            link(v_.memset(typ_t[:, NGROUP * GT:NG * GT], 0.0))
            link(v_.memset(idx_t[:, NGROUP * GT:NG * GT], 0))
            dve.wait_ge(consts_done, NCONST)

            def argmax_chunk(h, ch, q, k, i, in_sems):
                ng = HALF[h][1]
                dve.wait_ge(attr_in[q], in_sems)
                a = attr[0:ng, q, :, TYPE0:TYPE0 + R]
                link_in(k, i, 8, 4 * q, v_.tensor_reduce(out=amax[0:ng, q, :], in_=a, op=ALU.max, axis=AX.X))
                ins = v_.tensor_tensor(ahit[0:ng, :, :], a,
                                       amax[0:ng, q, :].rearrange("p (k u) -> p k u", u=1).to_broadcast([ng, CH, R]),
                                       ALU.is_equal)
                link_in(k, i, 8, 4 * q + 1, ins)
                ins = v_.tensor_tensor(ahit[0:ng, :, :], ahit[0:ng, :, :],
                                       rev_r[0:ng, :].rearrange("p (u r) -> p u r", u=1).to_broadcast([ng, CH, R]),
                                       ALU.mult)
                link_in(k, i, 8, 4 * q + 2, ins)
                dve.sem_inc(attr_used, 1)
                ins = v_.tensor_reduce(out=typ_g[h][0:ng, bass.ds(ch * CH, CH)], in_=ahit[0:ng, :, :], op=ALU.max,
                                       axis=AX.X)
                link_in(k, i, 8, 4 * q + 3, ins)

            def prepare(h):
                ng = HALF[h][1]
                d, s_, ty, re, fa, ix = (t[h][0:ng, :] for t in (dst_i, src_i, typ_g, rel_g, far_g, idx_g))
                link(v_.tensor_scalar(ty, ty, -1.0, float(R), ALU.mult, ALU.add))
                v_.tensor_copy(ix, s_)
                link(v_.tensor_copy(re, d))
                v_.scalar_tensor_tensor(out=fa, in0=re, scalar=PADDST / 2, in1=re, op0=ALU.is_lt, op1=ALU.mult)
                link(v_.scalar_tensor_tensor(out=ix, in0=ix, scalar=float(R), in1=ty, op0=ALU.mult, op1=ALU.add))
                v_.tensor_reduce(out=gmax[0:ng, h:h + 1], in_=fa, op=ALU.max, axis=AX.X)
                link(v_.tensor_reduce(out=gmin[0:ng, h:h + 1], in_=re, op=ALU.min, axis=AX.X))
                link(v_.tensor_scalar(fa, re, 1.0, None, ALU.add))
                link(v_.tensor_scalar(re, re, gmin[0:ng, h:h + 1], None, ALU.subtract))
                link(v_.scalar_tensor_tensor(out=fa, in0=re, scalar=float(W), in1=fa, op0=ALU.is_ge, op1=ALU.mult))
                v_.tensor_scalar(fa, fa, -1.0, None, ALU.add).then_inc(grouped, 1)

            dve.wait_ge(edges_in, 16 * 8)
            with dve.Fori(0, NCH // 2) as i:
                for q in range(2):
                    argmax_chunk(0, i * 2 + q, q, 0, i, i * 16 + 16)
            prepare(0)
            with dve.Fori(0, LASTCH // 2) as i:
                for q in range(2):
                    argmax_chunk(1, i * 2 + q, q, 1, i, i * 48 + (16 * (NCH // 2) + 48))
            with dve.Fori(LASTCH // 2, NCH // 2) as i:
                for q in range(2):
                    argmax_chunk(1, i * 2 + q, q, 1, i, i * 32 + (16 * (NCH // 2) + 16 * (LASTCH // 2) + 32))
            prepare(1)

            k = 0
            for h, (g0, ng) in enumerate(HALF):
                for tab in (rel_t, typ_t, far_t, idx_t):
                    for half in range(2):
                        dve.wait_ge(tr_ready, k + 1)
                        o = tab[:, g0 * GT:(g0 + ng) * GT].rearrange("e (g j) -> e j g", j=GT)
                        v_.tensor_copy(o[:, half * 4:half * 4 + 4, :],
                                       ps_look[:, k % 2, :].rearrange("e (j g) -> e j g", j=4)[:, :, 0:ng]
                                       ).then_inc(tr_taken, 1)
                        k += 1
            dve.wait_ge(tr_taken, k)
            dve.wait_ge(type_saved, 32)
            link(v_.memset(cnt[:, :], 0.0))
            dve.wait_ge(minmax_in, 32)
            G_ = NGROUP
            link(v_.tensor_copy(row_base[:, :], row_min[:, :]))
            link(v_.tensor_tensor(row_tmp[:, 0:G_], row_max[:, 0:G_], row_min[:, 0:G_], ALU.subtract))
            link(v_.tensor_reduce(out=flag[:, 0:1], in_=row_tmp[:, 0:G_], op=ALU.max, axis=AX.X))
            link(v_.tensor_scalar(flag[:, 1:2], flag[:, 0:1], float(W), None, ALU.is_ge))
            link(v_.tensor_tensor(row_tmp[:, 0:G_ - 1], row_min[:, 1:G_], row_max[:, 0:G_ - 1], ALU.is_ge))
            link(v_.tensor_reduce(out=flag[:, 2:3], in_=row_tmp[:, 0:G_ - 1], op=ALU.min, axis=AX.X))
            link(v_.tensor_tensor(row_tmp[:, 0:G_ - 3], row_min[:, 3:G_], row_min[:, 0:G_ - 3], ALU.subtract))
            link(v_.tensor_scalar(row_tmp[:, 0:G_ - 3], row_tmp[:, 0:G_ - 3], float(W), None, ALU.is_ge))
            link(v_.tensor_reduce(out=flag[:, 3:4], in_=row_tmp[:, 0:G_ - 3], op=ALU.min, axis=AX.X))
            first = row_min[:, 0:G_].rearrange("a (i u) -> a i u", u=U)[:, :, 0]
            link(v_.tensor_tensor(row_tmp[:, LAG:TURNS], first[:, LAG:TURNS], turn_min[:, LAG:TURNS], ALU.is_ge))
            link(v_.tensor_reduce(out=flag[:, 4:5], in_=row_tmp[:, LAG:TURNS], op=ALU.min, axis=AX.X))
            link(v_.tensor_scalar(flag[:, 5:6], flag[:, 1:2], 1.0, None, ALU.is_lt))
            link(v_.tensor_reduce(out=flag[:, 6:7], in_=flag[:, 2:6], op=ALU.min, axis=AX.X))
            link(v_.tensor_scalar(row_tmp[:, :], row_min[:, :], -float(SPARE), None, ALU.add))
            link(v_.tensor_scalar(row_tmp[:, :], row_tmp[:, :], flag[:, 6:7], float(SPARE), ALU.mult, ALU.add))
            link(v_.memset(row_tmp[:, G_:NG], float(SPARE)))
            link(v_.tensor_copy(row_count[:, :], row_tmp[:, :]))
            link(v_.tensor_copy(flag_i[:, 0:1], flag[:, 6:7]))
            link(v_.tensor_copy(flag_i[:, 1:2], flag[:, 1:2]))
            dve.sem_inc(flags_done, 1)
            dve.sem_inc(tables_done, 1)
            stream = dve.value_load(flag_i[0:1, 0:1], min_val=0, max_val=1)
            far = dve.value_load(flag_i[0:1, 1:2], min_val=0, max_val=1)

            def bc(ap, n, w):
                return ap.rearrange("p (n u) -> p n u", u=1).to_broadcast([P, n, w])

            def bc1(ap, n, w):
                return ap.rearrange("p (u w) -> p u w", u=1).to_broadcast([P, n, w])

            def make_hit(slot, g):
                return v_.tensor_tensor(hit[:, slot, :, :], bc1(iota_w[:, :], GT, W), bc(tiles(rel_t, g), GT, W),
                                        ALU.is_equal)

            def make_hit_typ(slot, g):
                return v_.tensor_tensor(hit_typ[:, slot, :, :], bc1(iota_r[:, :], GT, R), bc(tiles(typ_t, g), GT, R),
                                        ALU.is_equal)

            def count_window(row, g):
                return cnt[0:R, bass.ds(dve.value_load(row[0:1, bass.ds(g, 1)], min_val=0, max_val=SPARE), W)]

            NT = NGROUP * GT

            def far_windows(t):
                return v_.tensor_scalar(far_d[:, :], far0[:, :], -1.0, far_t[:, bass.ds(t, 1)], ALU.mult, ALU.add)

            with dve.If(stream < 1):
                with dve.Fori(0, NGROUP) as g:
                    make_hit(0, g)
                    make_hit_typ(0, g).then_inc(pre_hit, 1)
                    win = count_window(row_base, g)
                    dve.wait_ge(pre_done, g + 1)
                    dve.wait_ge(pre_ready, g + 1)
                    v_.tensor_tensor(win, counts, win, ALU.add).then_inc(pre_done, 1)
                with dve.If(far > 0):
                    with dve.Fori(0, NT) as t:
                        dve.wait_ge(far_v[0], t * (NFAR + 1) + 1)
                        v_.tensor_scalar(hit_typ[:, 0, 0, :], iota_r[:, :], typ_t[:, bass.ds(t, 1)], None,
                                         ALU.is_equal)
                        far_windows(t).then_inc(far_v[0], 1)
                        with dve.Fori(0, NFAR) as k:
                            dve.wait_ge(far_v[0], t * (NFAR + 1) + k + 2)
                            v_.tensor_scalar(far_hitb, iota_far[:, :], far_d[:, bass.ds(k, 1)], None,
                                             ALU.is_equal).then_inc(far_a[0], 1)
                            dve.wait_ge(far_b[0], t * NFAR + k + 1)
                            win = cnt[0:R, bass.ds(k * FARW, FARW)]
                            v_.tensor_tensor(win, ps_y[0][0:R, :], win, ALU.add).then_inc(far_v[0], 1)

            dve.wait_ge(root_done, NBLOCK + 1)
            for g in range(U):
                make_hit(g, g)
                make_hit_typ(g, g).then_inc(hit_ready, 1)
            for g in range(U):
                win = count_window(row_count, g)
                dve.wait_ge(cnt_ready, g + 1)
                if g:
                    dve.wait_ge(cnt_done, g)
                v_.tensor_tensor(win, counts, win, ALU.add).then_inc(cnt_done, 1)

            def type_onehot(q, full):
                dve.wait_ge(typ_in[q], full)
                v_.tensor_scalar(typ_oh[:, q, :], typ_oh[:, q, :], part[0:R, 0:1], None, ALU.is_equal
                                 ).then_inc(oh_ready, 1)

            def make_S(i, s):
                return v_.tensor_tensor(S[:, s % 2, :, :], hit[:, s, :, :], bc(tiles(c_t, i * U + s), GT, W),
                                        ALU.mult)

            def add_sums(l, i, s):
                g = i * U + s
                base = dve.value_load(row_base[0:1, bass.ds(g, 1)], min_val=0, max_val=N - 1)
                dve.wait_ge(agg_ready, g + (l * NGROUP + 1))
                dve.wait_ge(agg_done, g + (l * NGROUP + 1))
                win = acc[:, bass.ds(base, W)]
                v_.tensor_tensor(win, sums, win, ALU.add).then_inc(agg_done, 1)

            type_onehot(0, 16)
            with dve.Fori(0, TURNS) as i:
                for s in range(U):
                    g = i * U + s
                    if s:
                        add_sums(0, i, s - 1)
                    dve.wait_ge(look_ready, g + 1)
                    m = hit[:, s, :, :].rearrange("p (a b) w -> p a (b w)", a=2)
                    ins = v_.tensor_tensor(looked[:, :, :].rearrange("p (a b) w -> p a (b w)", a=2), m,
                                           ps_look[:, :, 0:4 * W], ALU.mult)
                    ins.then_inc(look_taken, 1)
                    dve.wait_ge(look_taken, g + 2)
                    link_in(2, i, 3 * U, 3 * s, v_.tensor_reduce(out=cnt_e[:, :], in_=looked[:, :, :], op=ALU.add,
                                                             axis=AX.X))
                    link_in(2, i, 3 * U, 3 * s + 1, v_.tensor_scalar(cnt_e[:, :], cnt_e[:, :], 1.0, None, ALU.max))
                    link_in(2, i, 3 * U, 3 * s + 2, v_.reciprocal(tiles(c_t, g), cnt_e[:, :]))
                    make_S(i, s).then_inc(S_ready, 1)
                    if s < U - 1:
                        type_onehot((s + 1) % 2, i * 32 + (16 * ((s + 1) // 2) + 16))
                    else:
                        with dve.If(i < TURNS - 1):
                            type_onehot(0, i * 32 + 48)
                    dve.wait_ge(S_ready, g + 1)
                    make_hit(s, g + U)
                    make_hit_typ(s, g + U).then_inc(hit_ready, 1)
                    win = count_window(row_count, g + U)
                    dve.wait_ge(cnt_ready, g + (U + 1))
                    dve.wait_ge(cnt_done, g + U)
                    v_.tensor_tensor(win, counts, win, ALU.add).then_inc(cnt_done, 1)
                add_sums(0, i, U - 1)

            def far_sums(l):
                v = far_v[2 + l]
                with dve.Fori(0, NT) as t:
                    dve.wait_ge(v, t * (NFAR + 1) + 1)
                    v_.tensor_copy(idx_s[:, 0, 0:1], idx_t[:, bass.ds(t, 1)]).then_inc(far_idx[l], 1)
                    far_windows(t).then_inc(v, 1)
                    with dve.Fori(0, NFAR) as k:
                        dve.wait_ge(v, t * (NFAR + 1) + k + 2)
                        v_.tensor_scalar(far_hit, iota_far[:, :], far_d[:, bass.ds(k, 1)],
                                         c_t[:, bass.ds(t, 1)], ALU.is_equal, ALU.mult).then_inc(far_a[2 + l], 1)
                        dve.wait_ge(far_b[2 + l], t * NFAR + k + 1)
                        win = acc[:, bass.ds(k * FARW, FARW)]
                        v_.tensor_tensor(win, ps_y[0][:, :], win, ALU.add).then_inc(v, 1)
                dve.wait_ge(v, NT * (NFAR + 1) + 1)

            dve.wait_ge(agg_done, NGROUP + 1)
            with dve.If(far > 0):
                with dve.Fori(0, NT) as t:
                    done = t * (NFAR + 6) + 1
                    dve.wait_ge(far_v[1], done)
                    dve.sem_inc(far_ask, 1)
                    far_windows(t).then_inc(far_v[1], 1)
                    dve.wait_ge(far_typ, t * 16 + 16)
                    v_.tensor_scalar(typ_oh[:, 0, 0:P], typ_oh[:, 0, 0:P], part[0:R, 0:1], None, ALU.is_equal
                                     ).then_inc(far_v[1], 1)
                    with dve.Fori(0, NFAR) as k:
                        dve.wait_ge(far_v[1], done + k + 2)
                        dve.sem_inc(far_a[1], 1)
                        dve.wait_ge(far_b[1], t * NFAR + k + 1)
                        v_.scalar_tensor_tensor(out=far_hit, in0=iota_far[:, :], scalar=far_d[:, bass.ds(k, 1)],
                                                in1=ps_y[0][:, :], op0=ALU.is_equal, op1=ALU.mult,
                                                accum_out=far_c[:, bass.ds(k, 1)]).then_inc(far_v[1], 1)
                    dve.wait_ge(far_v[1], done + (NFAR + 2))
                    v_.tensor_reduce(out=cnt_e[:, 0:1], in_=far_c[:, :], op=ALU.add, axis=AX.X).then_inc(far_v[1], 1)
                    dve.wait_ge(far_v[1], done + (NFAR + 3))
                    v_.tensor_scalar(cnt_e[:, 0:1], cnt_e[:, 0:1], 1.0, None, ALU.max).then_inc(far_v[1], 1)
                    dve.wait_ge(far_v[1], done + (NFAR + 4))
                    v_.reciprocal(cnt_e[:, 1:2], cnt_e[:, 0:1]).then_inc(far_v[1], 1)
                    dve.wait_ge(far_v[1], done + (NFAR + 5))
                    cc = c_t[:, bass.ds(t, 1)]
                    v_.tensor_tensor(cc, cc, cnt_e[:, 1:2], ALU.mult).then_inc(far_v[1], 1)
                dve.wait_ge(far_v[1], NT * (NFAR + 6) + 1)
                far_sums(0)
                dve.sem_inc(far_end, 1)

            dve.wait_ge(root_done, 2 * NBLOCK + 1)

            def residual(u, last=False):
                dve.wait_ge(fin_out, u + 1)
                dve.wait_ge(fin_ready, u + 2)
                dve.wait_ge(fin_x, u * 16 + (32 if last else 16))
                if last:
                    v_.tensor_tensor(z[:, 0, :], ps_fin[:, 0, :], x_in[:, 0, :], ALU.add)
                    v_.tensor_tensor(z[0:LASTN, 1, :], ps_fin[0:LASTN, 1, :], x_in[0:LASTN, 1, :], ALU.add
                                     ).then_inc(own_loop[4], 1)
                else:
                    v_.tensor_tensor(z, ps_fin, x_in[:, :, :], ALU.add).then_inc(own_loop[4], 1)
                dve.wait_ge(own_loop[4], u + 1)
                for q in range(2):
                    v_.bn_stats(stats[:, q, :], z[:, q, :]).then_inc(own_loop[5], 1)
                dve.wait_ge(own_loop[5], u * 2 + 2)
                dve.sem_inc(held, 1)
                v_.bn_aggr(mv[:, 0, :], stats[:, 0, :])
                v_.bn_aggr(mv[:, 1, :], stats[:, 1, :]).then_inc(fin_z, 1)

            def normalise(u):
                dve.wait_ge(fin_std, u + 1)
                v_.reciprocal(rstd[:, :], std[:, :]).then_inc(own_loop[6], 1)
                dve.wait_ge(own_loop[6], u + 1)
                for q in range(2):
                    ins = v_.tensor_scalar(zo[:, q, :], z[:, q, :], mv[:, q, 0:1], rstd[:, q:q + 1],
                                           ALU.subtract, ALU.mult)
                ins.then_inc(fin_out, 1)

            for start, end, behind in SPANS:
                with dve.Fori(start, end) as i:
                    for s in range(U):
                        g = i * U + s
                        dve.wait_ge(S_ready, g + (NGROUP - U + 1))
                        link_in(7, i, U, s, make_hit(s, g))
                        make_S(i, s).then_inc(S_ready, 1)
                        if s >= 1:
                            add_sums(1, i, s - 1)
                        if behind and s in (1, 2):
                            with dve.If(stream > 0):
                                if s == 1:
                                    residual(i - LAG)
                                else:
                                    normalise(i - LAG)
                    add_sums(1, i, U - 1)
            dve.wait_ge(agg_done, 2 * NGROUP + 1)
            with dve.If(far > 0):
                far_sums(1)
                dve.sem_inc(far_end, 1)
            with dve.If(stream < 1):
                with dve.Fori(0, TURNS - LAG) as u:
                    residual(u)
                    normalise(u)
            residual(NPAIR - 2)
            normalise(NPAIR - 2)
            residual(NPAIR - 1, last=True)
            normalise(NPAIR - 1)


_INS = ['x', 'src', 'dst', 'edge_attr_42', 'L0_gnn_w_rel1', 'L0_gnn_root1', 'L0_gnn_b1',
        'L0_gnn_w_rel2', 'L0_gnn_root2', 'L0_gnn_b2']


def kernel(**inputs):
    import numpy as _np
    import concourse.bacc as _bacc
    from concourse import mybir as _mybir
    from concourse.bass_utils import run_bass_kernel_spmd as _run

    nc = _bacc.Bacc("TRN2", target_bir_lowering=False, num_devices=1)
    arrays, args = {}, []
    for name in _INS:
        a = _np.ascontiguousarray(inputs[name])
        arrays[f"in_{name}_dram"] = a
        args.append(nc.dram_tensor(f"in_{name}_dram", a.shape, _mybir.dt.from_np(a.dtype), kind="ExternalInput").ap())
    out = nc.dram_tensor("out_0_dram", (N, C), F32, kind="ExternalOutput").ap()
    table1 = nc.dram_tensor("table1", (N * R, C), F32, kind="Internal").ap()
    table2 = nc.dram_tensor("table2", (N * R, C), F32, kind="Internal").ap()
    type_row = nc.dram_tensor("type_row", (NGROUP, GE), F32, kind="Internal").ap()
    row_scratch = nc.dram_tensor("row_scratch", (2, NGROUP), F32, kind="Internal").ap()
    gnn_kernel(nc, *args, out, table1, table2, type_row, row_scratch)
    r = _run(nc, [arrays], core_ids=[0])
    return r.results[0]["out_0_dram"]
```

```python
import concourse.bass as bass
from concourse import mybir
from contextlib import ExitStack


F32 = mybir.dt.float32
BF16 = mybir.dt.bfloat16
I32 = mybir.dt.int32
U32 = mybir.dt.uint32
ALU = mybir.AluOpType
ACT = mybir.ActivationFunctionType
AX = mybir.AxisListType

N = 12500
E = 200000
C = 128
R = 10
MSG = 42
TYPE0 = 16
P = 128
GT = 8
GE = GT * P
NGROUP = -(-E // GE)
GPAD = 4
NG = NGROUP + GPAD
W = 96
U = 4
TURNS = NGROUP // U
FARW = 512
NFAR = -(-N // FARW)
NCOL = NFAR * FARW
SPARE = N + 100
NBLOCK = -(-N // P)
NPAIR = NBLOCK // 2
LASTN = N - (NBLOCK - 1) * P
RC = R * C
YCHUNK = [(0, 512), (512, 512), (1024, 256)]
AHEAD = 3
LAG = 2
PADDST = 1.0e6
CH = 32
NCH = GE // CH
HALF = [(0, P), (P, NGROUP - P)]
LASTE = E - (NGROUP - 1) * GE
LASTCH = LASTE // CH
XR = 4
BREAK = 20
XTURNS = (NBLOCK - XR) // XR
EPS = 1e-5
assert TURNS * U == NGROUP and NPAIR * 2 == NBLOCK and LASTCH * CH == LASTE
assert TURNS == NPAIR and SPARE + W <= NCOL


def gnn_kernel(nc, x, src, dst, edge_attr, w_rel1, root1, b1, w_rel2, root2, b2, out, table1, table2,
               type_row, row_scratch):
    ctx = ExitStack()
    with ctx:
        def sb(name, shape, dt=F32):
            return ctx.enter_context(nc.sbuf_tensor(name, shape, dt))

        def sem(name):
            return ctx.enter_context(nc.semaphore(name))

        ident = sb("ident", [P, P])
        iota_w = sb("iota_w", [P, W])
        iota_far = sb("iota_far", [P, FARW])
        iota_r = sb("iota_r", [P, R])
        rev_r = sb("rev_r", [P, R])
        part = sb("part", [P, 1])
        far0 = sb("far0", [P, NFAR])
        turn_min = sb("turn_min", [1, TURNS])
        eps = sb("eps", [P, 1])
        wall = [sb(f"wall{l}", [P, R, C]) for l in range(2)]
        root = [sb(f"root{l}", [P, C]) for l in range(2)]
        bias = [sb(f"bias{l}", [P, 1]) for l in range(2)]
        rel_t = sb("rel_t", [P, NG * GT])
        typ_t = sb("typ_t", [P, NG * GT])
        far_t = sb("far_t", [P, NG * GT])
        idx_t = sb("idx_t", [P, NG * GT], U32)
        c_t = sb("c_t", [P, NG * GT])
        acc = sb("acc", [P, NCOL])
        cnt = sb("cnt", [P, NCOL])
        dst_i = [cnt[:, h * GE:(h + 1) * GE].bitcast(I32) for h in range(2)]
        src_i = [cnt[:, (2 + h) * GE:(3 + h) * GE].bitcast(I32) for h in range(2)]
        typ_g = [cnt[:, (4 + h) * GE:(5 + h) * GE] for h in range(2)]
        rel_g = [cnt[:, (6 + h) * GE:(7 + h) * GE] for h in range(2)]
        far_g = [cnt[:, (8 + h) * GE:(9 + h) * GE] for h in range(2)]
        idx_g = [cnt[:, (10 + h) * GE:(11 + h) * GE] for h in range(2)]
        attr_room = sb("attr_room", [P, 2 * CH * MSG])
        amax = sb("amax", [P, CH])
        ahit = sb("ahit", [P, CH, R])
        gmin = sb("gmin", [P, 2])
        gmax = sb("gmax", [P, 2])
        row_min = sb("row_min", [1, NG])
        row_max = sb("row_max", [1, NG])
        row_base = sb("row_base", [1, NG], I32)
        row_count = sb("row_count", [1, NG], I32)
        row_tmp = sb("row_tmp", [1, NG])
        flag = sb("flag", [1, 8])
        flag_i = sb("flag_i", [1, 2], I32)
        x_in = sb("x_in", [P, XR, C])
        h_s = sb("h_s", [P, 2, P])
        y_out = sb("y_out", [P, 2, RC])
        rows = sb("rows", [P, U, GT, C])
        idx_s = sb("idx_s", [P, U, GT], U32)
        hit = sb("hit", [P, U, GT, W], BF16)
        hit_typ = sb("hit_typ", [P, U, GT, R], BF16)
        typ_oh = sb("typ_oh", [R, 2, GE])
        cnt_e = sb("cnt_e", [P, GT])
        rows_room = rows[:, :, :, :].rearrange("p s j c -> p (s j c)")
        attr = [r[:, k * CH * MSG:(k + 1) * CH * MSG].rearrange("p (k m) -> p k m", m=MSG)
                for r in (attr_room, rows_room) for k in range(2)]
        z = y_out[:, 0, 0:2 * C].rearrange("p (q c) -> p q c", q=2)
        zo = y_out[:, 1, 0:2 * C].rearrange("p (q c) -> p q c", q=2)
        stats = sb("stats", [P, 2, 6])
        mv = sb("mv", [P, 2, 2])
        std = sb("std", [P, 2])
        rstd = sb("rstd", [P, 2])
        room = attr_room[:, :]
        S = room[:, 0:2 * GT * W].rearrange("p (q j w) -> p q j w", q=2, j=GT)
        looked = room[:, 2 * GT * W:3 * GT * W].rearrange("p (j w) -> p j w", j=GT)
        far_hit = room[:, 0:FARW]
        far_hitb = room[:, FARW:FARW + FARW // 2].bitcast(BF16)
        far_d = sb("far_d", [P, NFAR])
        far_c = sb("far_c", [P, NFAR])

        ps_look = ctx.enter_context(nc.psum_tensor("ps_look", [P, 2, 512], F32))
        ps_agg = ctx.enter_context(nc.psum_tensor("ps_agg", [P, 512], F32))
        ps_cnt = ctx.enter_context(nc.psum_tensor("ps_cnt", [P, 512], F32))
        ps_y = [ctx.enter_context(nc.psum_tensor(f"ps_y{k}", [P, 512], F32)) for k in range(3)]
        ps_root = ctx.enter_context(nc.psum_tensor("ps_root", [P, 512], F32))

        sums = ps_agg[:, 0:W]
        counts = ps_cnt[0:R, 0:W]
        ps_xt = [ps_cnt, ps_agg]
        ps_fin = ps_cnt[:, 0:2 * P].rearrange("p (q n) -> p q n", q=2)

        consts_done = sem("consts_done")
        weights_in = sem("weights_in")
        edges_in = sem("edges_in")
        pad_set = sem("pad_set")
        attr_in = [sem(f"attr_in{q}") for q in range(4)]
        attr_used = sem("attr_used")
        grouped = sem("grouped")
        type_saved = sem("type_saved")
        minmax_saved = sem("minmax_saved")
        minmax_in = sem("minmax_in")
        tr_ready = sem("tr_ready")
        tr_taken = sem("tr_taken")
        flags_done = sem("flags_done")
        tables_done = sem("tables_done")
        x_loaded = [sem(f"x_loaded{r}") for r in range(XR)]
        xt_ready = sem("xt_ready")
        xt_done = sem("xt_done")
        y_ready = sem("y_ready")
        y_taken = sem("y_taken")
        root_ready = sem("root_ready")
        root_done = sem("root_done")
        relu_done = sem("relu_done")
        y_stored = [[sem(f"y_stored{q}{k}") for k in range(len(YCHUNK))] for q in range(2)]
        idx_ready = sem("idx_ready")
        rows_in = [sem(f"rows_in{s}") for s in range(U)]
        typ_in = [sem(f"typ_in{q}") for q in range(2)]
        oh_ready = sem("oh_ready")
        look_ready = sem("look_ready")
        look_taken = sem("look_taken")
        hit_ready = sem("hit_ready")
        cnt_ready = sem("cnt_ready")
        cnt_done = sem("cnt_done")
        S_ready = sem("S_ready")
        agg_ready = sem("agg_ready")
        agg_done = sem("agg_done")
        own = sem("own")
        held = sem("held")
        own_loop = [sem(f"own_loop{k}") for k in range(8)]
        pre_hit = sem("pre_hit")
        pre_ready = sem("pre_ready")
        pre_done = sem("pre_done")
        fin_x = sem("fin_x")
        fin_copied = sem("fin_copied")
        fin_ready = sem("fin_ready")
        fin_z = sem("fin_z")
        fin_std = sem("fin_std")
        fin_out = sem("fin_out")
        fin_saved = sem("fin_saved")
        far_a = [sem(f"far_a{k}") for k in range(4)]
        far_b = [sem(f"far_b{k}") for k in range(4)]
        far_v = [sem(f"far_v{k}") for k in range(4)]
        far_idx = [sem(f"far_idx{k}") for k in range(2)]
        far_rows = [sem(f"far_rows{k}") for k in range(2)]
        far_ask = sem("far_ask")
        far_typ = sem("far_typ")
        far_end = sem("far_end")

        tables = [table1, table2]
        NCONST = 10

        def tiles(tab, g, n=1):
            return tab[:, bass.ds(g * GT, n * GT)]

        def store_chunk(eng, l, b, q, n, k):
            o, w = YCHUNK[k]
            view = tables[l].rearrange("(m r) c -> m (r c)", r=R)
            eng.dma_start(view[bass.ds(b * P, n), o:o + w], y_out[0:n, q, o:o + w]).then_inc(y_stored[q][k], 16)

        SPANS = [(0, LAG, False), (LAG, TURNS, True)]

        blk = ctx.enter_context(nc.Block())

        @blk.gpsimd
        def _(pool):
            g_ = nc.gpsimd
            g_.memset(ident[:], 0.0).then_inc(consts_done, 1)
            pool.wait_ge(consts_done, 1)
            g_.affine_select(out=ident[:], in_=ident[:], compare_op=ALU.not_equal, fill=1.0, base=0,
                             pattern=[[-1, P]], channel_multiplier=1).then_inc(consts_done, 1)
            for tile, step, base, mult in ((iota_w, 1, 0, 0), (iota_far, 1, 0, 0), (iota_r, 1, 0, 0),
                                           (rev_r, -1, R, 0), (part, 0, 0, 1), (far0, FARW, 0, 0)):
                g_.iota(tile[:], pattern=[[step, tile.shape[1]]], base=base, channel_multiplier=mult,
                        allow_small_or_imprecise_dtypes=True).then_inc(consts_done, 1)
            g_.iota(turn_min[:], pattern=[[U * P // 2, TURNS]], base=-(LAG - 1) * U * P // 2,
                    channel_multiplier=0, allow_small_or_imprecise_dtypes=True).then_inc(consts_done, 1)
            g_.memset(eps[:], EPS).then_inc(consts_done, 1)

            pool.wait_ge(pad_set, 3)
            for h, (g0, ng) in enumerate(HALF):
                full = ng if h == 0 else 64
                for ap, tile in ((dst, dst_i[h]), (src, src_i[h])):
                    pool.dma_start(tile[0:full, :], ap[g0 * GE:(g0 + full) * GE].rearrange("(g k) -> g k", k=GE)
                                   ).then_inc(edges_in, 16)
                    if full < ng:
                        pool.dma_start(tile[full:ng - 1, :], ap[(g0 + full) * GE:(g0 + ng - 1) * GE]
                                       .rearrange("(g k) -> g k", k=GE)).then_inc(edges_in, 16)
                        pool.dma_start(tile[ng - 1:ng, 0:LASTE], ap[E - LASTE:E].rearrange("(g k) -> g k", g=1)
                                       ).then_inc(edges_in, 16)

            def load_attr(h, q, ch, used, with_last):
                g0, ng = HALF[h]
                pool.wait_ge(attr_used, used)
                full = ng if h == 0 else 64
                parts = [(0, full)] if h == 0 else [(0, full), (full, ng - 1)]
                for a, b in parts:
                    view = edge_attr[(g0 + a) * GE:(g0 + b) * GE, :].rearrange("(g k) m -> g k m", k=GE)
                    pool.dma_start(attr[q][a:b, :, :], view[:, bass.ds(ch * CH, CH), :]).then_inc(attr_in[q], 16)
                if h == 1:
                    if with_last:
                        view = edge_attr[E - LASTE:E, :].rearrange("(g k) m -> g k m", g=1)
                        pool.dma_start(attr[q][ng - 1:ng, :, :], view[:, bass.ds(ch * CH, CH), :]
                                       ).then_inc(attr_in[q], 16)

            with pool.Fori(0, NCH // 4) as i:
                for q in range(4):
                    load_attr(0, q, i * 4 + q, i * 4 + (q + 1), False)
            with pool.Fori(0, LASTCH // 4) as i:
                for q in range(4):
                    load_attr(1, q, i * 4 + q, i * 4 + (NCH + q + 1), True)
            for ch in range(LASTCH // 4 * 4, LASTCH // 4 * 4 + 4):
                load_attr(1, ch % 4, ch, NCH + ch + 1, ch < LASTCH)
            with pool.Fori(LASTCH // 4 + 1, NCH // 4) as i:
                for q in range(4):
                    load_attr(1, q, i * 4 + q, i * 4 + (NCH + q + 1), False)

            for h, (g0, ng) in enumerate(HALF):
                pool.wait_ge(grouped, h + 1)
                for k, col in enumerate((gmin, gmax)):
                    pool.dma_start(row_scratch[k:k + 1, g0:g0 + ng].rearrange("k g -> g k"), col[0:ng, h:h + 1]
                                   ).then_inc(minmax_saved, 16)
                pool.dma_start(type_row[g0:g0 + ng, :], typ_g[h][0:ng, :]).then_inc(type_saved, 16)
            pool.wait_ge(minmax_saved, 64)
            pool.dma_start(row_min[0:1, 0:NGROUP], row_scratch[0:1, 0:NGROUP]).then_inc(minmax_in, 16)
            pool.dma_start(row_max[0:1, 0:NGROUP], row_scratch[1:2, 0:NGROUP]).then_inc(minmax_in, 16)

            for l in range(2):
                for stored in y_stored[0] + y_stored[1]:
                    pool.wait_ge(stored, 16 * NPAIR * (l + 1))
                with pool.Fori(0, TURNS) as i:
                    for s in range(U):
                        pool.wait_ge(idx_ready, i * U + (l * NG + s + 1))
                        pool.sem_inc(held, 1)
                        for j in range(GT):
                            pool.indirect_dma_start(
                                out=rows[:, s, j, :], out_offset=None, in_=tables[l][:, :],
                                in_offset=bass.IndirectOffsetOnAxis(ap=idx_s[:, s, j:j + 1], axis=0)
                            ).then_inc(rows_in[s], 16)
                far = pool.value_load(flag_i[0:1, 1:2], min_val=0, max_val=1)
                with pool.If(far > 0):
                    with pool.Fori(0, NGROUP * GT) as t:
                        pool.wait_ge(far_idx[l], t + 1)
                        pool.sem_inc(held, 1)
                        pool.indirect_dma_start(
                            out=rows[:, 0, 0, :], out_offset=None, in_=tables[l][:, :],
                            in_offset=bass.IndirectOffsetOnAxis(ap=idx_s[:, 0, 0:1], axis=0)
                        ).then_inc(far_rows[l], 16)

        @blk.sync
        def _(sp):
            for l, (w, r, b) in enumerate(((w_rel1, root1, b1), (w_rel2, root2, b2))):
                sp.dma_start(wall[l][:, :, :], w.rearrange("r d o -> d r o")).then_inc(weights_in, 16)
                sp.dma_start(root[l][:, :], r[:, :]).then_inc(weights_in, 16)
                sp.dma_start(bias[l][:, :], b.rearrange("(o u) -> o u", u=1)).then_inc(weights_in, 16)

            def load_x(b, r):
                n = LASTN if isinstance(b, int) and b == NBLOCK - 1 else P
                sp.dma_start(x_in[0:n, r, :], x[bass.ds(b * P, n), :]).then_inc(x_loaded[r], 16)

            def store_rows(b, q, n):
                for k in range(len(YCHUNK)):
                    sp.wait_ge(y_taken, b * 3 + (k + 4))
                    store_chunk(sp, 0, b, q, n, k)

            for r in range(XR):
                load_x(r, r)
            with sp.Fori(0, XTURNS) as w:
                for r in range(XR):
                    sp.wait_ge(xt_ready, w * XR + (r + 1))
                    load_x(w * XR + (r + XR), r)
                    store_rows(w * XR + r, r % 2, P)
            for b in range(XTURNS * XR, NBLOCK):
                if b + XR < NBLOCK:
                    sp.wait_ge(xt_ready, b + 1)
                    load_x(b + XR, b % XR)
                store_rows(b, b % 2, LASTN if b == NBLOCK - 1 else P)

            def load_types(g, q, freed):
                if freed is not None:
                    sp.wait_ge(look_ready, freed)
                sp.dma_start(typ_oh[:, q, :], type_row[bass.ds(g, 1), :].to_broadcast([R, GE])
                             ).then_inc(typ_in[q], 16)

            sp.wait_ge(type_saved, 32)
            load_types(0, 0, None)
            load_types(1, 1, None)
            with sp.Fori(0, TURNS - 1) as i:
                for s in range(U):
                    load_types(i * U + (s + 2), s % 2, i * U + (s + 1))
            for s in range(U - 2):
                load_types((TURNS - 1) * U + s + 2, s % 2, (TURNS - 1) * U + s + 1)
            sp.wait_ge(flags_done, 1)
            far = sp.value_load(flag_i[0:1, 1:2], min_val=0, max_val=1)
            with sp.If(far > 0):
                flat = type_row.rearrange("g k -> (g k)")
                with sp.Fori(0, NGROUP * GT) as t:
                    sp.wait_ge(far_ask, t + 1)
                    sp.dma_start(typ_oh[:, 0, 0:P],
                                 flat[bass.ds(t * P, P)].rearrange("(u k) -> u k", u=1).to_broadcast([R, P])
                                 ).then_inc(far_typ, 16)

            def fin_io(u, last, first):
                if not first:
                    sp.wait_ge(fin_z, u + 1)
                    sp.sem_inc(held, 1)
                    sp.wait_ge(fin_saved, u * 16)
                    sp.sem_inc(held, 1)
                if last:
                    sp.dma_start(x_in[:, 0, :], x[(NBLOCK - 2) * P:(NBLOCK - 1) * P, :]).then_inc(fin_x, 16)
                    sp.dma_start(x_in[0:LASTN, 1, :], x[(NBLOCK - 1) * P:N, :]).then_inc(fin_x, 16)
                else:
                    sp.dma_start(x_in[:, 0:2, :], x[bass.ds(u * (2 * P), 2 * P), :]
                                 .rearrange("(q p) c -> p q c", q=2)).then_inc(fin_x, 16)
                sp.wait_ge(fin_out, u + 2)
                if last:
                    sp.dma_start(out[(NBLOCK - 2) * P:(NBLOCK - 1) * P, :], zo[:, 0, :]).then_inc(fin_saved, 16)
                    sp.dma_start(out[(NBLOCK - 1) * P:N, :], zo[0:LASTN, 1, :]).then_inc(fin_saved, 16)
                else:
                    sp.dma_start(out[bass.ds(u * (2 * P), 2 * P), :].rearrange("(q p) c -> p q c", q=2),
                                 zo[:, :, :]).then_inc(fin_saved, 16)

            for stored in y_stored[0] + y_stored[1]:
                sp.wait_ge(stored, 16 * NPAIR * 2)
            fin_io(0, False, True)
            with sp.Fori(1, NPAIR - 1) as u:
                fin_io(u, False, False)
            fin_io(NPAIR - 1, True, False)
            sp.wait_ge(fin_saved, 16 * (NPAIR + 1))

        @blk.scalar
        def _(act):
            a_ = nc.scalar

            def take_xt(b, q, n, used):
                act.wait_ge(xt_ready, b + 1)
                if used is not None:
                    act.wait_ge(root_ready, used)
                a_.copy(h_s[:, q, 0:n], ps_xt[q][:, 0:n]).then_inc(xt_done, 1)

            def take_block(l, u, q, n, first=False):
                b = u * 2 + q
                bt = b + l * NBLOCK
                for k, (o, w) in enumerate(YCHUNK):
                    act.wait_ge(y_ready, bt * 3 + (k + 1))
                    if not first:
                        act.wait_ge(y_stored[q][k], (u + l * NPAIR) * 16)
                    a_.copy(y_out[0:n, q, o:o + w], ps_y[k][0:n, 0:w]).then_inc(y_taken, 1)
                act.wait_ge(root_ready, bt + 1)
                a_.activation(acc[:, bass.ds(b * P, n)], ps_root[:, 0:n], ACT.Identity,
                              bias=bias[l][:, 0:1]).then_inc(root_done, 1)
                if l == 1:
                    act.wait_ge(y_taken, bt * 3 + 6)
                    for k in range(len(YCHUNK)):
                        store_chunk(act, l, b, q, n, k)

            act.wait_ge(weights_in, 16 * 6)
            take_xt(0, 0, P, None)
            take_xt(1, 1, P, None)
            for q in range(2):
                take_block(0, 0, q, P, first=True)
                take_xt(2 + q, q, P, q + 1)
            with act.Fori(1, NPAIR - 2) as u:
                for q in range(2):
                    take_block(0, u, q, P)
                    take_xt(u * 2 + (2 + q), q, P, u * 2 + (q + 1))
            for q in range(2):
                take_block(0, NPAIR - 2, q, P)
                take_xt(NBLOCK - 2 + q, q, LASTN if q else P, NBLOCK - 3 + q)
            for q in range(2):
                take_block(0, NPAIR - 1, q, LASTN if q else P)

            act.wait_ge(tables_done, 1)
            stream = act.value_load(flag_i[0:1, 0:1], min_val=0, max_val=1)
            far = act.value_load(flag_i[0:1, 1:2], min_val=0, max_val=1)

            def give_indices(g, s):
                a_.copy(idx_s[:, s, :], tiles(idx_t, g)).then_inc(idx_ready, 1)

            def next_indices(l, i, s):
                act.wait_ge(agg_ready, i * U + (l * NGROUP + s + 1))
                give_indices(i * U + (U + s), s)

            def relu(u, last=False):
                n = P + LASTN if last else 2 * P
                a_.activation(h_s[:, :, :].rearrange("p q n -> p (q n)")[:, 0:n], acc[:, bass.ds(u * (2 * P), n)],
                              ACT.Relu).then_inc(relu_done, 1)

            def pair(u, last=False):
                relu(u, last)
                for q in range(2):
                    take_block(1, u, q, LASTN if (last and q) else P)

            for s in range(U):
                give_indices(s, s)
            for start, end, behind in SPANS:
                with act.Fori(start, end) as i:
                    for s in range(U):
                        next_indices(0, i, s)
                        if behind and s in (0, 2):
                            with act.If(stream > 0):
                                if s == 0:
                                    act.wait_ge(agg_done, i * U + 1)
                                    relu(i - LAG)
                                take_block(1, i - LAG, s // 2, P)
            act.wait_ge(agg_done, NGROUP + 1)
            with act.If(far > 0):
                act.wait_ge(far_end, 1)
            with act.If(stream < 1):
                with act.Fori(0, TURNS - LAG) as u:
                    pair(u)
            pair(NPAIR - 2)
            pair(NPAIR - 1, last=True)

            def copy_pair(u, last=False):
                n = P + LASTN if last else 2 * P
                act.wait_ge(fin_ready, u + 1)
                a_.copy(h_s[:, :, :].rearrange("p q n -> p (q n)")[:, 0:n], acc[:, bass.ds(u * (2 * P), n)]
                        ).then_inc(fin_copied, 1)

            def root_of_variance(u):
                act.wait_ge(fin_z, u + 2)
                a_.activation(std[:, :], mv[:, :, 1], ACT.Sqrt, bias=eps[:, 0:1]).then_inc(fin_std, 1)

            for s in range(U):
                give_indices(s, s)
            for start, end, behind in SPANS:
                with act.Fori(start, end) as i:
                    for s in range(U):
                        next_indices(1, i, s)
                        if behind and s < 2:
                            with act.If(stream > 0):
                                if s == 0:
                                    act.wait_ge(agg_done, i * U + (NGROUP + 1))
                                    copy_pair(i - LAG)
                                else:
                                    root_of_variance(i - LAG)
            act.wait_ge(agg_done, 2 * NGROUP + 1)
            with act.If(far > 0):
                act.wait_ge(far_end, 2)
            with act.If(stream < 1):
                with act.Fori(0, TURNS - LAG) as u:
                    copy_pair(u)
                    root_of_variance(u)
            copy_pair(NPAIR - 2)
            root_of_variance(NPAIR - 2)
            copy_pair(NPAIR - 1, last=True)
            root_of_variance(NPAIR - 1)

        @blk.tensor
        def _(pe):
            t_ = nc.tensor

            def turn_x(w, r, n=P, first=False):
                w, r = w + r // XR, r % XR
                q = r % 2
                pe.wait_ge(x_loaded[r], w * 16 + 16)
                if not first:
                    pe.wait_ge(xt_done, w * XR + (r - 1))
                t_.transpose(ps_xt[q][:, 0:n], x_in[0:n, r, :], ident[0:n, 0:n]).then_inc(xt_ready, 1)

            def make_block(l, u, q, n, mid=None):
                b = u * 2 + q
                bt = b + l * NBLOCK
                h = h_s[:, q, 0:n]
                w = wall[l][:, :, :].rearrange("d r o -> d (r o)")
                for k, (o, wid) in enumerate(YCHUNK):
                    pe.wait_ge(y_taken, bt * 3 + (k + 1))
                    t_.matmul(ps_y[k][0:n, 0:wid], lhsT=h, rhs=w[:, o:o + wid], start=True, stop=True
                              ).then_inc(y_ready, 1)
                pe.wait_ge(root_done, bt + 1)
                t_.matmul(ps_root[:, 0:n], lhsT=root[l][:, :], rhs=h, start=True, stop=True
                          ).then_inc(root_ready, 1)

            pe.wait_ge(consts_done, NCONST)
            pe.wait_ge(weights_in, 16 * 6)
            turn_x(0, 0, first=True)
            turn_x(0, 1, first=True)

            def table_block(w, r, n=P, ahead=P):
                pe.wait_ge(xt_done, w * XR + (r + 1))
                make_block(0, w * 2 + r // 2, r % 2, n)
                if ahead:
                    turn_x(w, r + 2, ahead)

            def first_table(start, end):
                with pe.Fori(start, end) as w:
                    for r in range(XR):
                        table_block(w, r)

            first_table(0, BREAK)
            k = 0
            for h, (g0, ng) in enumerate(HALF):
                pe.wait_ge(grouped, h + 1)
                for tab in (rel_g, typ_g, far_g, idx_g):
                    for half in range(2):
                        if k >= 2:
                            pe.wait_ge(tr_taken, k - 1)
                        for j in range(4):
                            e0 = (half * 4 + j) * P
                            last = t_.transpose(ps_look[:, k % 2, j * P:j * P + ng], tab[h][0:ng, e0:e0 + P],
                                                ident[0:ng, 0:ng])
                        last.then_inc(tr_ready, 1)
                        k += 1

            first_table(BREAK, XTURNS)
            for b in range(XTURNS * XR, NBLOCK):
                table_block(b // XR, b % XR, LASTN if b == NBLOCK - 1 else P,
                            0 if b + 2 >= NBLOCK else LASTN if b + 2 == NBLOCK - 1 else P)

            pe.wait_ge(flags_done, 1)
            stream = pe.value_load(flag_i[0:1, 0:1], min_val=0, max_val=1)
            far = pe.value_load(flag_i[0:1, 1:2], min_val=0, max_val=1)

            def count(slot):
                for j in range(GT):
                    last = t_.matmul(counts, lhsT=hit_typ[:, slot, j, :], rhs=hit[:, slot, j, :],
                                     start=(j == 0), stop=(j == GT - 1))
                return last

            with pe.If(stream < 1):
                with pe.Fori(0, NGROUP) as g:
                    pe.wait_ge(pre_hit, g + 1)
                    count(0).then_inc(pre_ready, 1)
                with pe.If(far > 0):
                    with pe.Fori(0, NGROUP * GT) as t:
                        with pe.Fori(0, NFAR) as k:
                            pe.wait_ge(far_a[0], t * NFAR + k + 1)
                            t_.matmul(ps_y[0][0:R, :], lhsT=hit_typ[:, 0, 0, :], rhs=far_hitb, start=True,
                                      stop=True).then_inc(far_b[0], 1)

            def make_counts(g, s):
                pe.wait_ge(hit_ready, g + 1)
                pe.wait_ge(cnt_done, g + 1)
                count(s).then_inc(cnt_ready, 1)

            def look_up(g, s):
                base = pe.value_load(row_base[0:1, bass.ds(g, 1)], min_val=0, max_val=N - 1)
                pe.wait_ge(oh_ready, g + 1)
                pe.wait_ge(look_taken, g + 1)
                pe.wait_ge(cnt_done, g + 3)
                for j in range(GT):
                    last = t_.matmul(ps_look[:, j // 4, (j % 4) * W:(j % 4 + 1) * W],
                                     lhsT=typ_oh[:, s % 2, j * P:(j + 1) * P],
                                     rhs=cnt[0:R, bass.ds(base, W)], start=True, stop=True)
                last.then_inc(look_ready, 1)

            for g in range(AHEAD):
                make_counts(g, g)
            look_up(0, 0)

            def aggregate(l, i, s):
                pe.wait_ge(S_ready, i * U + (l * NGROUP + s + 1))
                pe.wait_ge(rows_in[s], i * (16 * GT) + (16 * GT * (l * TURNS + 1)))
                pe.wait_ge(agg_done, i * U + (l * NGROUP + s + 1))
                for j in range(GT):
                    last = t_.matmul(sums, lhsT=rows[:, s, j, :], rhs=S[:, s % 2, j, :],
                                     start=(j == 0), stop=(j == GT - 1))
                last.then_inc(agg_ready, 1)

            for start, end, behind in SPANS:
                with pe.Fori(start, end) as i:
                    for s in range(U):
                        g = i * U + s
                        make_counts(g + AHEAD, (s + AHEAD) % U)
                        if s < U - 1:
                            look_up(g + 1, s + 1)
                        else:
                            with pe.If(i < TURNS - 1):
                                look_up(g + 1, s + 1)
                        aggregate(0, i, s)
                        if behind and s in (0, 2):
                            with pe.If(stream > 0):
                                if s == 0:
                                    pe.wait_ge(relu_done, i - (LAG - 1))
                                make_block(1, i - LAG, s // 2, P)
            with pe.If(far > 0):
                with pe.Fori(0, NGROUP * GT) as t:
                    with pe.Fori(0, NFAR) as k:
                        pe.wait_ge(far_a[1], t * NFAR + k + 1)
                        t_.matmul(ps_y[0][:, :], lhsT=typ_oh[:, 0, 0:P], rhs=cnt[0:R, bass.ds(k * FARW, FARW)],
                                  start=True, stop=True).then_inc(far_b[1], 1)

            def far_sums(l):
                with pe.Fori(0, NGROUP * GT) as t:
                    with pe.Fori(0, NFAR) as k:
                        pe.wait_ge(far_rows[l], t * 16 + 16)
                        pe.wait_ge(far_a[2 + l], t * NFAR + k + 1)
                        t_.matmul(ps_y[0][:, :], lhsT=rows[:, 0, 0, :], rhs=far_hit, start=True,
                                  stop=True).then_inc(far_b[2 + l], 1)

            with pe.If(far > 0):
                far_sums(0)
            with pe.If(stream < 1):
                with pe.Fori(0, TURNS - LAG) as u:
                    pe.wait_ge(relu_done, u + 1)
                    for q in range(2):
                        make_block(1, u, q, P)
            for u in (NPAIR - 2, NPAIR - 1):
                pe.wait_ge(relu_done, u + 1)
                for q in range(2):
                    make_block(1, u, q, LASTN if (u == NPAIR - 1 and q) else P)

            def turn_pair(u, last=False):
                pe.wait_ge(fin_z, u + 1)
                pe.wait_ge(fin_copied, u + 1)
                for q in range(2):
                    n = LASTN if (last and q) else P
                    ins = t_.transpose(ps_fin[0:n, q, :], h_s[:, q, 0:n], ident[:, :])
                ins.then_inc(fin_ready, 1)

            for start, end, behind in SPANS:
                with pe.Fori(start, end) as i:
                    for s in range(U):
                        aggregate(1, i, s)
                        if behind and s == 0:
                            with pe.If(stream > 0):
                                turn_pair(i - LAG)
            with pe.If(far > 0):
                far_sums(1)
            with pe.If(stream < 1):
                with pe.Fori(0, TURNS - LAG) as u:
                    turn_pair(u)
            turn_pair(NPAIR - 2)
            turn_pair(NPAIR - 1, last=True)

        @blk.vector
        def _(dve):
            v_ = nc.vector
            steps = [0]

            def link(ins):
                steps[0] += 1
                ins.then_inc(own, 1)
                dve.wait_ge(own, steps[0])

            def link_in(k, i, per, n, ins):
                ins.then_inc(own_loop[k], 1)
                dve.wait_ge(own_loop[k], i * per + (n + 1))

            dve.sem_inc(y_taken, 3)
            dve.sem_inc(root_done, 1)
            dve.sem_inc(look_taken, 1)
            dve.sem_inc(agg_done, 1)
            dve.sem_inc(attr_used, 4)
            for credited in (pre_done, cnt_done, fin_ready, fin_z, fin_out, *far_v):
                dve.sem_inc(credited, 1)

            v_.memset(dst_i[1][64:HALF[1][1], :], int(PADDST)).then_inc(pad_set, 1)
            v_.memset(src_i[1][64:HALF[1][1], :], 0).then_inc(pad_set, 1)
            v_.memset(acc[:, N:NCOL], 0.0).then_inc(pad_set, 1)
            link(v_.memset(row_min[:, :], float(N)))
            link(v_.memset(row_max[:, :], float(N)))
            npt = GPAD * GT
            link(v_.memset(rel_t[:, NGROUP * GT:NG * GT], PADDST))
            link(v_.memset(typ_t[:, NGROUP * GT:NG * GT], 0.0))
            link(v_.memset(idx_t[:, NGROUP * GT:NG * GT], 0))
            dve.wait_ge(consts_done, NCONST)

            def argmax_chunk(h, ch, q, k, i, in_sems):
                ng = HALF[h][1]
                dve.wait_ge(attr_in[q], in_sems)
                a = attr[q][0:ng, :, TYPE0:TYPE0 + R]
                link_in(k, i, 16, 4 * q, v_.tensor_reduce(out=amax[0:ng, :], in_=a, op=ALU.max, axis=AX.X))
                ins = v_.tensor_tensor(ahit[0:ng, :, :], a,
                                       amax[0:ng, :].rearrange("p (k u) -> p k u", u=1).to_broadcast([ng, CH, R]),
                                       ALU.is_equal)
                link_in(k, i, 16, 4 * q + 1, ins)
                ins = v_.tensor_tensor(ahit[0:ng, :, :], ahit[0:ng, :, :],
                                       rev_r[0:ng, :].rearrange("p (u r) -> p u r", u=1).to_broadcast([ng, CH, R]),
                                       ALU.mult)
                link_in(k, i, 16, 4 * q + 2, ins)
                dve.sem_inc(attr_used, 1)
                ins = v_.tensor_reduce(out=typ_g[h][0:ng, bass.ds(ch * CH, CH)], in_=ahit[0:ng, :, :], op=ALU.max,
                                       axis=AX.X)
                link_in(k, i, 16, 4 * q + 3, ins)

            def prepare(h):
                ng = HALF[h][1]
                d, s_, ty, re, fa, ix = (t[h][0:ng, :] for t in (dst_i, src_i, typ_g, rel_g, far_g, idx_g))
                link(v_.tensor_scalar(ty, ty, -1.0, float(R), ALU.mult, ALU.add))
                v_.tensor_copy(ix, s_)
                link(v_.tensor_copy(re, d))
                v_.scalar_tensor_tensor(out=fa, in0=re, scalar=PADDST / 2, in1=re, op0=ALU.is_lt, op1=ALU.mult)
                link(v_.scalar_tensor_tensor(out=ix, in0=ix, scalar=float(R), in1=ty, op0=ALU.mult, op1=ALU.add))
                v_.tensor_reduce(out=gmax[0:ng, h:h + 1], in_=fa, op=ALU.max, axis=AX.X)
                link(v_.tensor_reduce(out=gmin[0:ng, h:h + 1], in_=re, op=ALU.min, axis=AX.X))
                link(v_.tensor_scalar(fa, re, 1.0, None, ALU.add))
                link(v_.tensor_scalar(re, re, gmin[0:ng, h:h + 1], None, ALU.subtract))
                link(v_.scalar_tensor_tensor(out=fa, in0=re, scalar=float(W), in1=fa, op0=ALU.is_ge, op1=ALU.mult))
                v_.tensor_scalar(fa, fa, -1.0, None, ALU.add).then_inc(grouped, 1)

            dve.wait_ge(edges_in, 16 * 8)
            with dve.Fori(0, NCH // 4) as i:
                for q in range(4):
                    argmax_chunk(0, i * 4 + q, q, 0, i, i * 16 + 16)
            prepare(0)

            def arrived(n, q):
                lasts = sum(1 for ch in range(n * 4) if ch % 4 == q and ch < LASTCH)
                return 16 * (NCH // 4) + 32 * n + 16 * lasts

            with dve.Fori(0, LASTCH // 4) as i:
                for q in range(4):
                    argmax_chunk(1, i * 4 + q, q, 1, i, i * 48 + (arrived(0, q) + 48))
            n = LASTCH // 4
            for q in range(4):
                argmax_chunk(1, n * 4 + q, q, 1, n, arrived(n + 1, q))
            with dve.Fori(n + 1, NCH // 4) as i:
                for q in range(4):
                    argmax_chunk(1, i * 4 + q, q, 1, i, i * 32 + (arrived(n + 1, q) - 32 * n))
            prepare(1)

            k = 0
            for h, (g0, ng) in enumerate(HALF):
                for tab in (rel_t, typ_t, far_t, idx_t):
                    for half in range(2):
                        dve.wait_ge(tr_ready, k + 1)
                        o = tab[:, g0 * GT:(g0 + ng) * GT].rearrange("e (g j) -> e j g", j=GT)
                        v_.tensor_copy(o[:, half * 4:half * 4 + 4, :],
                                       ps_look[:, k % 2, :].rearrange("e (j g) -> e j g", j=4)[:, :, 0:ng]
                                       ).then_inc(tr_taken, 1)
                        k += 1
            dve.wait_ge(tr_taken, k)
            dve.wait_ge(type_saved, 32)
            link(v_.memset(cnt[:, :], 0.0))
            dve.wait_ge(minmax_in, 32)
            G_ = NGROUP
            link(v_.tensor_copy(row_base[:, :], row_min[:, :]))
            link(v_.tensor_tensor(row_tmp[:, 0:G_], row_max[:, 0:G_], row_min[:, 0:G_], ALU.subtract))
            link(v_.tensor_reduce(out=flag[:, 0:1], in_=row_tmp[:, 0:G_], op=ALU.max, axis=AX.X))
            link(v_.tensor_scalar(flag[:, 1:2], flag[:, 0:1], float(W), None, ALU.is_ge))
            link(v_.tensor_tensor(row_tmp[:, 0:G_ - 1], row_min[:, 1:G_], row_max[:, 0:G_ - 1], ALU.is_ge))
            link(v_.tensor_reduce(out=flag[:, 2:3], in_=row_tmp[:, 0:G_ - 1], op=ALU.min, axis=AX.X))
            link(v_.tensor_tensor(row_tmp[:, 0:G_ - 2], row_min[:, 2:G_], row_min[:, 0:G_ - 2], ALU.subtract))
            link(v_.tensor_scalar(row_tmp[:, 0:G_ - 2], row_tmp[:, 0:G_ - 2], float(W), None, ALU.is_ge))
            link(v_.tensor_reduce(out=flag[:, 3:4], in_=row_tmp[:, 0:G_ - 2], op=ALU.min, axis=AX.X))
            first = row_min[:, 0:G_].rearrange("a (i u) -> a i u", u=U)[:, :, 0]
            link(v_.tensor_tensor(row_tmp[:, LAG:TURNS], first[:, LAG:TURNS], turn_min[:, LAG:TURNS], ALU.is_ge))
            link(v_.tensor_reduce(out=flag[:, 4:5], in_=row_tmp[:, LAG:TURNS], op=ALU.min, axis=AX.X))
            link(v_.tensor_scalar(flag[:, 5:6], flag[:, 1:2], 1.0, None, ALU.is_lt))
            link(v_.tensor_reduce(out=flag[:, 6:7], in_=flag[:, 2:6], op=ALU.min, axis=AX.X))
            link(v_.tensor_scalar(row_tmp[:, :], row_min[:, :], -float(SPARE), None, ALU.add))
            link(v_.tensor_scalar(row_tmp[:, :], row_tmp[:, :], flag[:, 6:7], float(SPARE), ALU.mult, ALU.add))
            link(v_.memset(row_tmp[:, G_:NG], float(SPARE)))
            link(v_.tensor_copy(row_count[:, :], row_tmp[:, :]))
            link(v_.tensor_copy(flag_i[:, 0:1], flag[:, 6:7]))
            link(v_.tensor_copy(flag_i[:, 1:2], flag[:, 1:2]))
            dve.sem_inc(flags_done, 1)
            dve.sem_inc(tables_done, 1)
            stream = dve.value_load(flag_i[0:1, 0:1], min_val=0, max_val=1)
            far = dve.value_load(flag_i[0:1, 1:2], min_val=0, max_val=1)

            def bc(ap, n, w):
                return ap.rearrange("p (n u) -> p n u", u=1).to_broadcast([P, n, w])

            def bc1(ap, n, w):
                return ap.rearrange("p (u w) -> p u w", u=1).to_broadcast([P, n, w])

            def make_hit(slot, g):
                return v_.tensor_tensor(hit[:, slot, :, :], bc1(iota_w[:, :], GT, W), bc(tiles(rel_t, g), GT, W),
                                        ALU.is_equal)

            def make_hit_typ(slot, g):
                return v_.tensor_tensor(hit_typ[:, slot, :, :], bc1(iota_r[:, :], GT, R), bc(tiles(typ_t, g), GT, R),
                                        ALU.is_equal)

            def count_window(row, g):
                return cnt[0:R, bass.ds(dve.value_load(row[0:1, bass.ds(g, 1)], min_val=0, max_val=SPARE), W)]

            NT = NGROUP * GT

            def far_windows(t):
                return v_.tensor_scalar(far_d[:, :], far0[:, :], -1.0, far_t[:, bass.ds(t, 1)], ALU.mult, ALU.add)

            with dve.If(stream < 1):
                with dve.Fori(0, NGROUP) as g:
                    make_hit(0, g)
                    make_hit_typ(0, g).then_inc(pre_hit, 1)
                    win = count_window(row_base, g)
                    dve.wait_ge(pre_done, g + 1)
                    dve.wait_ge(pre_ready, g + 1)
                    v_.tensor_tensor(win, counts, win, ALU.add).then_inc(pre_done, 1)
                with dve.If(far > 0):
                    with dve.Fori(0, NT) as t:
                        dve.wait_ge(far_v[0], t * (NFAR + 1) + 1)
                        v_.tensor_scalar(hit_typ[:, 0, 0, :], iota_r[:, :], typ_t[:, bass.ds(t, 1)], None,
                                         ALU.is_equal)
                        far_windows(t).then_inc(far_v[0], 1)
                        with dve.Fori(0, NFAR) as k:
                            dve.wait_ge(far_v[0], t * (NFAR + 1) + k + 2)
                            v_.tensor_scalar(far_hitb, iota_far[:, :], far_d[:, bass.ds(k, 1)], None,
                                             ALU.is_equal).then_inc(far_a[0], 1)
                            dve.wait_ge(far_b[0], t * NFAR + k + 1)
                            win = cnt[0:R, bass.ds(k * FARW, FARW)]
                            v_.tensor_tensor(win, ps_y[0][0:R, :], win, ALU.add).then_inc(far_v[0], 1)

            dve.wait_ge(root_done, NBLOCK + 1)
            for g in range(U):
                make_hit(g, g)
                make_hit_typ(g, g).then_inc(hit_ready, 1)

            def add_counts(g):
                win = count_window(row_count, g)
                dve.wait_ge(cnt_ready, g + 1)
                dve.wait_ge(cnt_done, g + 1)
                v_.tensor_tensor(win, counts, win, ALU.add).then_inc(cnt_done, 1)

            for g in range(AHEAD):
                add_counts(g)

            def type_onehot(q, full):
                dve.wait_ge(typ_in[q], full)
                v_.tensor_scalar(typ_oh[:, q, :], typ_oh[:, q, :], part[0:R, 0:1], None, ALU.is_equal
                                 ).then_inc(oh_ready, 1)

            def make_S(i, s):
                return v_.tensor_tensor(S[:, s % 2, :, :], hit[:, s, :, :], bc(tiles(c_t, i * U + s), GT, W),
                                        ALU.mult)

            def add_sums(l, i, s):
                g = i * U + s
                base = dve.value_load(row_base[0:1, bass.ds(g, 1)], min_val=0, max_val=N - 1)
                dve.wait_ge(agg_ready, g + (l * NGROUP + 1))
                dve.wait_ge(agg_done, g + (l * NGROUP + 1))
                win = acc[:, bass.ds(base, W)]
                v_.tensor_tensor(win, sums, win, ALU.add).then_inc(agg_done, 1)

            type_onehot(0, 16)
            type_onehot(1, 16)
            with dve.Fori(0, TURNS) as i:
                for s in range(U):
                    g = i * U + s
                    dve.wait_ge(look_ready, g + 1)
                    m = hit[:, s, :, :].rearrange("p (a b) w -> p a (b w)", a=2)
                    ins = v_.tensor_tensor(looked[:, :, :].rearrange("p (a b) w -> p a (b w)", a=2), m,
                                           ps_look[:, :, 0:4 * W], ALU.mult)
                    ins.then_inc(look_taken, 1)
                    dve.wait_ge(look_taken, g + 2)
                    link_in(2, i, 3 * U, 3 * s, v_.tensor_reduce(out=cnt_e[:, :], in_=looked[:, :, :], op=ALU.add,
                                                                 axis=AX.X))
                    link_in(2, i, 3 * U, 3 * s + 1, v_.tensor_scalar(cnt_e[:, :], cnt_e[:, :], 1.0, None, ALU.max))
                    link_in(2, i, 3 * U, 3 * s + 2, v_.reciprocal(tiles(c_t, g), cnt_e[:, :]))
                    make_S(i, s).then_inc(S_ready, 1)
                    if s < U - 2:
                        type_onehot(s % 2, i * 32 + (16 * (s // 2) + 32))
                    else:
                        with dve.If(i < TURNS - 1):
                            type_onehot(s % 2, i * 32 + (16 * (s // 2) + 32))
                    if s:
                        add_sums(0, i, s - 1)
                    dve.wait_ge(S_ready, g + 1)
                    make_hit(s, g + U)
                    make_hit_typ(s, g + U).then_inc(hit_ready, 1)
                    add_counts(g + AHEAD)
                add_sums(0, i, U - 1)

            def far_sums(l):
                v = far_v[2 + l]
                with dve.Fori(0, NT) as t:
                    dve.wait_ge(v, t * (NFAR + 1) + 1)
                    v_.tensor_copy(idx_s[:, 0, 0:1], idx_t[:, bass.ds(t, 1)]).then_inc(far_idx[l], 1)
                    far_windows(t).then_inc(v, 1)
                    with dve.Fori(0, NFAR) as k:
                        dve.wait_ge(v, t * (NFAR + 1) + k + 2)
                        v_.tensor_scalar(far_hit, iota_far[:, :], far_d[:, bass.ds(k, 1)],
                                         c_t[:, bass.ds(t, 1)], ALU.is_equal, ALU.mult).then_inc(far_a[2 + l], 1)
                        dve.wait_ge(far_b[2 + l], t * NFAR + k + 1)
                        win = acc[:, bass.ds(k * FARW, FARW)]
                        v_.tensor_tensor(win, ps_y[0][:, :], win, ALU.add).then_inc(v, 1)
                dve.wait_ge(v, NT * (NFAR + 1) + 1)

            dve.wait_ge(agg_done, NGROUP + 1)
            with dve.If(far > 0):
                with dve.Fori(0, NT) as t:
                    done = t * (NFAR + 6) + 1
                    dve.wait_ge(far_v[1], done)
                    dve.sem_inc(far_ask, 1)
                    far_windows(t).then_inc(far_v[1], 1)
                    dve.wait_ge(far_typ, t * 16 + 16)
                    v_.tensor_scalar(typ_oh[:, 0, 0:P], typ_oh[:, 0, 0:P], part[0:R, 0:1], None, ALU.is_equal
                                     ).then_inc(far_v[1], 1)
                    with dve.Fori(0, NFAR) as k:
                        dve.wait_ge(far_v[1], done + k + 2)
                        dve.sem_inc(far_a[1], 1)
                        dve.wait_ge(far_b[1], t * NFAR + k + 1)
                        v_.scalar_tensor_tensor(out=far_hit, in0=iota_far[:, :], scalar=far_d[:, bass.ds(k, 1)],
                                                in1=ps_y[0][:, :], op0=ALU.is_equal, op1=ALU.mult,
                                                accum_out=far_c[:, bass.ds(k, 1)]).then_inc(far_v[1], 1)
                    dve.wait_ge(far_v[1], done + (NFAR + 2))
                    v_.tensor_reduce(out=cnt_e[:, 0:1], in_=far_c[:, :], op=ALU.add, axis=AX.X).then_inc(far_v[1], 1)
                    dve.wait_ge(far_v[1], done + (NFAR + 3))
                    v_.tensor_scalar(cnt_e[:, 0:1], cnt_e[:, 0:1], 1.0, None, ALU.max).then_inc(far_v[1], 1)
                    dve.wait_ge(far_v[1], done + (NFAR + 4))
                    v_.reciprocal(cnt_e[:, 1:2], cnt_e[:, 0:1]).then_inc(far_v[1], 1)
                    dve.wait_ge(far_v[1], done + (NFAR + 5))
                    cc = c_t[:, bass.ds(t, 1)]
                    v_.tensor_tensor(cc, cc, cnt_e[:, 1:2], ALU.mult).then_inc(far_v[1], 1)
                dve.wait_ge(far_v[1], NT * (NFAR + 6) + 1)
                far_sums(0)
                dve.sem_inc(far_end, 1)

            dve.wait_ge(root_done, 2 * NBLOCK + 1)

            def residual(u, last=False):
                dve.wait_ge(fin_out, u + 1)
                dve.wait_ge(fin_ready, u + 2)
                dve.wait_ge(fin_x, u * 16 + (32 if last else 16))
                if last:
                    v_.tensor_tensor(z[:, 0, :], ps_fin[:, 0, :], x_in[:, 0, :], ALU.add)
                    v_.tensor_tensor(z[0:LASTN, 1, :], ps_fin[0:LASTN, 1, :], x_in[0:LASTN, 1, :], ALU.add
                                     ).then_inc(own_loop[4], 1)
                else:
                    v_.tensor_tensor(z, ps_fin, x_in[:, 0:2, :], ALU.add).then_inc(own_loop[4], 1)
                dve.wait_ge(own_loop[4], u + 1)
                for q in range(2):
                    v_.bn_stats(stats[:, q, :], z[:, q, :]).then_inc(own_loop[5], 1)
                dve.wait_ge(own_loop[5], u * 2 + 2)
                dve.sem_inc(held, 1)
                v_.bn_aggr(mv[:, 0, :], stats[:, 0, :])
                v_.bn_aggr(mv[:, 1, :], stats[:, 1, :]).then_inc(fin_z, 1)

            def normalise(u):
                dve.wait_ge(fin_std, u + 1)
                v_.reciprocal(rstd[:, :], std[:, :]).then_inc(own_loop[6], 1)
                dve.wait_ge(own_loop[6], u + 1)
                for q in range(2):
                    ins = v_.tensor_scalar(zo[:, q, :], z[:, q, :], mv[:, q, 0:1], rstd[:, q:q + 1],
                                           ALU.subtract, ALU.mult)
                ins.then_inc(fin_out, 1)

            for start, end, behind in SPANS:
                with dve.Fori(start, end) as i:
                    for s in range(U):
                        g = i * U + s
                        dve.wait_ge(S_ready, g + (NGROUP - U + 1))
                        link_in(7, i, U, s, make_hit(s, g))
                        make_S(i, s).then_inc(S_ready, 1)
                        if s >= 1:
                            add_sums(1, i, s - 1)
                        if behind and s in (1, 2):
                            with dve.If(stream > 0):
                                if s == 1:
                                    residual(i - LAG)
                                else:
                                    normalise(i - LAG)
                    add_sums(1, i, U - 1)
            dve.wait_ge(agg_done, 2 * NGROUP + 1)
            with dve.If(far > 0):
                far_sums(1)
                dve.sem_inc(far_end, 1)
            with dve.If(stream < 1):
                with dve.Fori(0, TURNS - LAG) as u:
                    residual(u)
                    normalise(u)
            residual(NPAIR - 2)
            normalise(NPAIR - 2)
            residual(NPAIR - 1, last=True)
            normalise(NPAIR - 1)


_INS = ['x', 'src', 'dst', 'edge_attr_42', 'L0_gnn_w_rel1', 'L0_gnn_root1', 'L0_gnn_b1',
        'L0_gnn_w_rel2', 'L0_gnn_root2', 'L0_gnn_b2']


def kernel(**inputs):
    import numpy as _np
    import concourse.bacc as _bacc
    from concourse import mybir as _mybir
    from concourse.bass_utils import run_bass_kernel_spmd as _run

    nc = _bacc.Bacc("TRN2", target_bir_lowering=False, num_devices=1)
    arrays, args = {}, []
    for name in _INS:
        a = _np.ascontiguousarray(inputs[name])
        arrays[f"in_{name}_dram"] = a
        args.append(nc.dram_tensor(f"in_{name}_dram", a.shape, _mybir.dt.from_np(a.dtype), kind="ExternalInput").ap())
    out = nc.dram_tensor("out_0_dram", (N, C), F32, kind="ExternalOutput").ap()
    table1 = nc.dram_tensor("table1", (N * R, C), F32, kind="Internal").ap()
    table2 = nc.dram_tensor("table2", (N * R, C), F32, kind="Internal").ap()
    type_row = nc.dram_tensor("type_row", (NGROUP, GE), F32, kind="Internal").ap()
    row_scratch = nc.dram_tensor("row_scratch", (2, NGROUP), F32, kind="Internal").ap()
    gnn_kernel(nc, *args, out, table1, table2, type_row, row_scratch)
    r = _run(nc, [arrays], core_ids=[0])
    return r.results[0]["out_0_dram"]
```

```python
import concourse.bass as bass
from concourse import mybir
from contextlib import ExitStack


F32 = mybir.dt.float32
BF16 = mybir.dt.bfloat16
I32 = mybir.dt.int32
U32 = mybir.dt.uint32
ALU = mybir.AluOpType
ACT = mybir.ActivationFunctionType
AX = mybir.AxisListType

N = 12500
E = 200000
C = 128
R = 10
MSG = 42
TYPE0 = 16
P = 128
GT = 8
GE = GT * P
NGROUP = -(-E // GE)
GPAD = 2 * 4
NG = NGROUP + GPAD
W = 96
U = 4
TURNS = NGROUP // U
FARW = 512
NFAR = -(-N // FARW)
NCOL = NFAR * FARW
SPARE = N + 100
NBLOCK = -(-N // P)
NPAIR = NBLOCK // 2
LASTN = N - (NBLOCK - 1) * P
RC = R * C
YCHUNK = [(0, 512), (512, 512), (1024, 256)]
AHEAD = 3
LAG = 2
PADDST = 1.0e6
HALF = [(0, P), (P, NGROUP - P)]
LASTE = E - (NGROUP - 1) * GE
LASTP = LASTE // GT
TE = U * GE
XR = 4
XTURNS = (NBLOCK - XR) // XR
EPS = 1e-5
assert TURNS * U == NGROUP and NPAIR * 2 == NBLOCK and LASTP * GT == LASTE
assert TURNS == NPAIR and SPARE + W <= NCOL


def gnn_kernel(nc, x, src, dst, edge_attr, w_rel1, root1, b1, w_rel2, root2, b2, out, table1, table2,
               type_row, row_scratch):
    ctx = ExitStack()
    with ctx:
        def sb(name, shape, dt=F32):
            return ctx.enter_context(nc.sbuf_tensor(name, shape, dt))

        def sem(name):
            return ctx.enter_context(nc.semaphore(name))

        ident = sb("ident", [P, P])
        iota_w = sb("iota_w", [P, W])
        iota_far = sb("iota_far", [P, FARW])
        iota_r = sb("iota_r", [P, R])
        rev_r = sb("rev_r", [P, R])
        part = sb("part", [P, 1])
        far0 = sb("far0", [P, NFAR])
        turn_min = sb("turn_min", [1, TURNS])
        eps = sb("eps", [P, 1])
        root = [sb(f"root{l}", [P, C]) for l in range(2)]
        bias = [sb(f"bias{l}", [P, 1]) for l in range(2)]
        rel_t = sb("rel_t", [P, NG * GT])
        typ_t = sb("typ_t", [P, NG * GT])
        far_t = sb("far_t", [P, NG * GT])
        idx_t = sb("idx_t", [P, NG * GT], U32)
        c_t = sb("c_t", [P, NG * GT])
        acc = sb("acc", [P, NCOL])
        cnt = sb("cnt", [P, NCOL])
        dst_i = [cnt[:, h * GE:(h + 1) * GE].bitcast(I32) for h in range(2)]
        dst_f = [cnt[:, (2 + h) * GE:(3 + h) * GE] for h in range(2)]
        dst_m = [cnt[:, (4 + h) * GE:(5 + h) * GE] for h in range(2)]
        dst_e = cnt[:, 6 * GE:6 * GE + NG * GT].bitcast(I32)
        attr = sb("attr", [P, U * GT, MSG])
        amax = sb("amax", [P, U * GT])
        ahit = sb("ahit", [P, U * GT, R])
        gmin = sb("gmin", [P, 2])
        gmax = sb("gmax", [P, 2])
        base_all = sb("base_all", [P, NGROUP])
        row_min = sb("row_min", [1, NG])
        row_max = sb("row_max", [1, NG])
        row_base = sb("row_base", [1, NG], I32)
        row_count = sb("row_count", [1, NG], I32)
        row_tmp = sb("row_tmp", [1, NG])
        flag = sb("flag", [1, 8])
        flag_i = sb("flag_i", [1, 2], I32)
        x_in = sb("x_in", [P, XR, C])
        h_s = sb("h_s", [P, 2, P])
        y_out = sb("y_out", [P, 2, RC])
        rows = sb("rows", [P, U, GT, C])
        wall = [rows[:, 0:2, :, :].rearrange("p s j c -> p (s j) c")[:, 0:R, :], sb("wall1", [P, R, C])]
        idx_s = sb("idx_s", [P, U, GT], U32)
        hit = sb("hit", [P, U, GT, W], BF16)
        hit_typ = sb("hit_typ", [P, U, GT, R], BF16)
        typ_oh = sb("typ_oh", [R, 2, GE])
        cnt_e = sb("cnt_e", [P, GT])
        z = y_out[:, 0, 0:2 * C].rearrange("p (q c) -> p q c", q=2)
        zo = y_out[:, 1, 0:2 * C].rearrange("p (q c) -> p q c", q=2)
        stats = sb("stats", [P, 2, 6])
        mv = sb("mv", [P, 2, 2])
        std = sb("std", [P, 2])
        rstd = sb("rstd", [P, 2])
        room = sb("room", [P, 3 * GT * W])
        S = room[:, 0:2 * GT * W].rearrange("p (q j w) -> p q j w", q=2, j=GT)
        looked = room[:, 2 * GT * W:3 * GT * W].rearrange("p (j w) -> p j w", j=GT)
        far_hit = room[:, 0:FARW]
        far_hitb = room[:, FARW:FARW + FARW // 2].bitcast(BF16)
        far_d = sb("far_d", [P, NFAR])
        far_c = sb("far_c", [P, NFAR])

        ps_look = ctx.enter_context(nc.psum_tensor("ps_look", [P, 2, 512], F32))
        ps_agg = ctx.enter_context(nc.psum_tensor("ps_agg", [P, 512], F32))
        ps_cnt = ctx.enter_context(nc.psum_tensor("ps_cnt", [P, 512], F32))
        ps_y = [ctx.enter_context(nc.psum_tensor(f"ps_y{k}", [P, 512], F32)) for k in range(3)]
        ps_root = ctx.enter_context(nc.psum_tensor("ps_root", [P, 512], F32))

        sums = ps_agg[:, 0:W]
        counts = ps_cnt[0:R, 0:W]
        ps_xt = [ps_cnt, ps_agg]
        ps_fin = ps_cnt[:, 0:2 * P].rearrange("p (q n) -> p q n", q=2)

        consts_done = sem("consts_done")
        weights_in = [sem(f"weights_in{l}") for l in range(2)]
        groups_in = sem("groups_in")
        edges_in = sem("edges_in")
        pad_set = sem("pad_set")
        first_attr = sem("first_attr")
        attr_in = sem("attr_in")
        attr_used = sem("attr_used")
        typed = sem("typed")
        grouped = sem("grouped")
        first_saved = sem("first_saved")
        type_saved = sem("type_saved")
        minmax_saved = sem("minmax_saved")
        minmax_in = sem("minmax_in")
        pre_attr = sem("pre_attr")
        pre_typed = sem("pre_typed")
        flags_done = sem("flags_done")
        x_loaded = [sem(f"x_loaded{r}") for r in range(XR)]
        xt_ready = sem("xt_ready")
        xt_done = sem("xt_done")
        y_ready = sem("y_ready")
        y_taken = sem("y_taken")
        root_ready = sem("root_ready")
        root_done = sem("root_done")
        relu_done = sem("relu_done")
        y_stored = [[sem(f"y_stored{q}{k}") for k in range(len(YCHUNK))] for q in range(2)]
        idx_ready = sem("idx_ready")
        rows_in = [sem(f"rows_in{s}") for s in range(U)]
        typ_in = [sem(f"typ_in{q}") for q in range(2)]
        oh_ready = sem("oh_ready")
        look_ready = sem("look_ready")
        look_taken = sem("look_taken")
        hit_ready = sem("hit_ready")
        cnt_ready = sem("cnt_ready")
        cnt_done = sem("cnt_done")
        S_ready = sem("S_ready")
        agg_ready = sem("agg_ready")
        agg_done = sem("agg_done")
        own = sem("own")
        held = sem("held")
        own_loop = [sem(f"own_loop{k}") for k in range(8)]
        pre_hit = sem("pre_hit")
        pre_ready = sem("pre_ready")
        pre_done = sem("pre_done")
        fin_x = sem("fin_x")
        fin_copied = sem("fin_copied")
        fin_ready = sem("fin_ready")
        fin_z = sem("fin_z")
        fin_std = sem("fin_std")
        fin_out = sem("fin_out")
        fin_saved = sem("fin_saved")
        far_a = [sem(f"far_a{k}") for k in range(4)]
        far_b = [sem(f"far_b{k}") for k in range(4)]
        far_v = [sem(f"far_v{k}") for k in range(4)]
        far_idx = [sem(f"far_idx{k}") for k in range(2)]
        far_rows = [sem(f"far_rows{k}") for k in range(2)]
        far_ask = sem("far_ask")
        far_typ = sem("far_typ")
        far_end = sem("far_end")

        tables = [table1, table2]
        NCONST = 10

        def tiles(tab, g, n=1):
            return tab[:, bass.ds(g * GT, n * GT)]

        def load_attr(eng, i, last=False, done=None):
            done = attr_in if done is None else done
            full = U - 1 if last else U
            view = edge_attr[bass.ds(i * TE, full * GE), :].rearrange("(s p j) m -> p s (j m)", p=P, j=GT)
            tile = attr[:, :, :].rearrange("p (s j) m -> p s (j m)", j=GT)
            eng.dma_start(tile[:, 0:full, :], view).then_inc(done, 16)
            if last:
                view = edge_attr[E - LASTE:E, :].rearrange("(p j) m -> p (j m)", j=GT)
                eng.dma_start(tile[0:LASTP, U - 1, :], view).then_inc(done, 16)

        def save_types(eng, i, done=None):
            eng.dma_start(type_row[bass.ds(i * U, U), :].rearrange("s (p j) -> p s j", j=GT),
                          typ_t[:, bass.ds(i * U * GT, U * GT)].rearrange("p (s j) -> p s j", j=GT)
                          ).then_inc(type_saved if done is None else done, 16)

        def load_weights(eng, l, w, r, b):
            eng.dma_start(wall[l][:, :, :], w.rearrange("r d o -> d r o")).then_inc(weights_in[l], 16)
            eng.dma_start(root[l][:, :], r[:, :]).then_inc(weights_in[l], 16)
            eng.dma_start(bias[l][:, :], b.rearrange("(o u) -> o u", u=1)).then_inc(weights_in[l], 16)

        def store_chunk(eng, l, b, q, n, k):
            o, w = YCHUNK[k]
            view = tables[l].rearrange("(m r) c -> m (r c)", r=R)
            eng.dma_start(view[bass.ds(b * P, n), o:o + w], y_out[0:n, q, o:o + w]).then_inc(y_stored[q][k], 16)

        SPANS = [(0, LAG, False), (LAG, TURNS, True)]

        blk = ctx.enter_context(nc.Block())

        @blk.gpsimd
        def _(pool):
            g_ = nc.gpsimd
            g_.memset(ident[:], 0.0).then_inc(consts_done, 1)
            pool.wait_ge(consts_done, 1)
            g_.affine_select(out=ident[:], in_=ident[:], compare_op=ALU.not_equal, fill=1.0, base=0,
                             pattern=[[-1, P]], channel_multiplier=1).then_inc(consts_done, 1)
            for tile, step, base, mult in ((iota_w, 1, 0, 0), (iota_far, 1, 0, 0), (iota_r, 1, 0, 0),
                                           (rev_r, -1, R, 0), (part, 0, 0, 1), (far0, FARW, 0, 0)):
                g_.iota(tile[:], pattern=[[step, tile.shape[1]]], base=base, channel_multiplier=mult,
                        allow_small_or_imprecise_dtypes=True).then_inc(consts_done, 1)
            g_.iota(turn_min[:], pattern=[[U * P // 2, TURNS]], base=-(LAG - 1) * U * P // 2,
                    channel_multiplier=0, allow_small_or_imprecise_dtypes=True).then_inc(consts_done, 1)
            g_.memset(eps[:], EPS).then_inc(consts_done, 1)

            pool.wait_ge(pad_set, 4)
            for h, (g0, ng) in enumerate(HALF):
                full = ng if h == 0 else 64
                pool.dma_start(dst_i[h][0:full, :], dst[g0 * GE:(g0 + full) * GE].rearrange("(g k) -> g k", k=GE)
                               ).then_inc(groups_in, 16)
                if full < ng:
                    pool.dma_start(dst_i[h][full:ng - 1, :], dst[(g0 + full) * GE:(g0 + ng - 1) * GE]
                                   .rearrange("(g k) -> g k", k=GE)).then_inc(groups_in, 16)
                    pool.dma_start(dst_i[h][ng - 1:ng, 0:LASTE], dst[E - LASTE:E].rearrange("(g k) -> g k", g=1)
                                   ).then_inc(groups_in, 16)
            for h, (g0, ng) in enumerate(HALF):
                pool.wait_ge(grouped, h + 1)
                for k, col in enumerate((gmin, gmax)):
                    pool.dma_start(row_scratch[k:k + 1, g0:g0 + ng].rearrange("k g -> g k"), col[0:ng, h:h + 1]
                                   ).then_inc(minmax_saved, 16)
            pool.wait_ge(minmax_saved, 64)
            pool.dma_start(row_min[0:1, 0:NGROUP], row_scratch[0:1, 0:NGROUP]).then_inc(minmax_in, 16)
            pool.dma_start(row_max[0:1, 0:NGROUP], row_scratch[1:2, 0:NGROUP]).then_inc(minmax_in, 16)
            pool.dma_start(base_all[:, :], row_scratch[0:1, 0:NGROUP].to_broadcast([P, NGROUP])
                           ).then_inc(minmax_in, 16)
            pool.wait_ge(flags_done, 1)
            stream = pool.value_load(flag_i[0:1, 0:1], min_val=0, max_val=1)
            with pool.If(stream < 1):
                with pool.Fori(0, TURNS - 1) as i:
                    pool.wait_ge(pre_typed, i + 1)
                    load_attr(pool, i, done=pre_attr)
                pool.wait_ge(pre_typed, TURNS)
                load_attr(pool, TURNS - 1, last=True, done=pre_attr)
                pool.wait_ge(pre_typed, TURNS + 1)
            load_attr(pool, 0, done=first_attr)
            pool.wait_ge(attr_used, 1)
            load_attr(pool, 1, done=first_attr)
            pool.wait_ge(typed, 1)
            save_types(pool, 0, first_saved)

            for l in range(2):
                for stored in y_stored[0] + y_stored[1]:
                    pool.wait_ge(stored, 16 * NPAIR * (l + 1))
                with pool.Fori(0, TURNS) as i:
                    for s in range(U):
                        pool.wait_ge(idx_ready, i * U + (l * (NGROUP + U) + s + 1))
                        pool.sem_inc(held, 1)
                        for j in range(GT):
                            pool.indirect_dma_start(
                                out=rows[:, s, j, :], out_offset=None, in_=tables[l][:, :],
                                in_offset=bass.IndirectOffsetOnAxis(ap=idx_s[:, s, j:j + 1], axis=0)
                            ).then_inc(rows_in[s], 16)
                far = pool.value_load(flag_i[0:1, 1:2], min_val=0, max_val=1)
                with pool.If(far > 0):
                    with pool.Fori(0, NGROUP * GT) as t:
                        pool.wait_ge(far_idx[l], t + 1)
                        pool.sem_inc(held, 1)
                        pool.indirect_dma_start(
                            out=rows[:, 0, 0, :], out_offset=None, in_=tables[l][:, :],
                            in_offset=bass.IndirectOffsetOnAxis(ap=idx_s[:, 0, 0:1], axis=0)
                        ).then_inc(far_rows[l], 16)

        @blk.sync
        def _(sp):
            def load_x(b, r):
                n = LASTN if isinstance(b, int) and b == NBLOCK - 1 else P
                sp.dma_start(x_in[0:n, r, :], x[bass.ds(b * P, n), :]).then_inc(x_loaded[r], 16)

            def store_rows(b, q, n):
                for k in range(len(YCHUNK)):
                    sp.wait_ge(y_taken, b * 3 + (k + 4))
                    store_chunk(sp, 0, b, q, n, k)

            for r in range(XR):
                load_x(r, r)
                if r == 1:
                    load_weights(sp, 0, w_rel1, root1, b1)
            sp.wait_ge(pad_set, 4)
            for ap, tile in ((dst, dst_e), (src, idx_t[:, :].bitcast(I32))):
                whole = (NGROUP - 1) * GE
                sp.dma_start(tile[:, 0:(NGROUP - 1) * GT].rearrange("p (g j) -> p g j", j=GT),
                             ap[0:whole].rearrange("(g p j) -> p g j", p=P, j=GT)).then_inc(edges_in, 16)
                sp.dma_start(tile[0:LASTP, (NGROUP - 1) * GT:NGROUP * GT],
                             ap[whole:E].rearrange("(p j) -> p j", j=GT)).then_inc(edges_in, 16)
            with sp.Fori(0, XTURNS) as w:
                for r in range(XR):
                    sp.wait_ge(xt_ready, w * XR + (r + 1))
                    load_x(w * XR + (r + XR), r)
                    store_rows(w * XR + r, r % 2, P)
            for b in range(XTURNS * XR, NBLOCK):
                if b + XR < NBLOCK:
                    sp.wait_ge(xt_ready, b + 1)
                    load_x(b + XR, b % XR)
                store_rows(b, b % 2, LASTN if b == NBLOCK - 1 else P)

            def load_types(g, q, freed):
                if freed is not None:
                    sp.wait_ge(look_ready, freed)
                sp.dma_start(typ_oh[:, q, :], type_row[bass.ds(g, 1), :].to_broadcast([R, GE])
                             ).then_inc(typ_in[q], 16)

            def serve_turn(i, types=U, save=True, attr=True, last=False):
                for s in range(types):
                    if s == 2:
                        sp.wait_ge(type_saved, i * 16 + 16)
                    load_types(i * U + (s + 2), s % 2, i * U + (s + 1))
                if save:
                    sp.wait_ge(typed, i + 3)
                    save_types(sp, i + 2)
                if attr:
                    load_attr(sp, i + 3, last=last)

            sp.wait_ge(typed, 2)
            save_types(sp, 1)
            load_attr(sp, 2)
            sp.wait_ge(first_saved, 16)
            load_types(0, 0, None)
            load_types(1, 1, None)
            with sp.Fori(0, TURNS - 4) as i:
                serve_turn(i)
            serve_turn(TURNS - 4, last=True)
            serve_turn(TURNS - 3, attr=False)
            serve_turn(TURNS - 2, save=False, attr=False)
            serve_turn(TURNS - 1, types=2, save=False, attr=False)
            far = sp.value_load(flag_i[0:1, 1:2], min_val=0, max_val=1)
            with sp.If(far > 0):
                with sp.Fori(0, NGROUP) as g:
                    sp.wait_ge(far_ask, g + 1)
                    sp.dma_start(typ_oh[:, 0, :], type_row[bass.ds(g, 1), :].to_broadcast([R, GE])
                                 ).then_inc(far_typ, 16)

            def fin_io(u, last, first):
                if not first:
                    sp.wait_ge(fin_z, u + 1)
                    sp.sem_inc(held, 1)
                    sp.wait_ge(fin_saved, u * 16)
                    sp.sem_inc(held, 1)
                if last:
                    sp.dma_start(x_in[:, 0, :], x[(NBLOCK - 2) * P:(NBLOCK - 1) * P, :]).then_inc(fin_x, 16)
                    sp.dma_start(x_in[0:LASTN, 1, :], x[(NBLOCK - 1) * P:N, :]).then_inc(fin_x, 16)
                else:
                    sp.dma_start(x_in[:, 0:2, :], x[bass.ds(u * (2 * P), 2 * P), :]
                                 .rearrange("(q p) c -> p q c", q=2)).then_inc(fin_x, 16)
                sp.wait_ge(fin_out, u + 2)
                if last:
                    sp.dma_start(out[(NBLOCK - 2) * P:(NBLOCK - 1) * P, :], zo[:, 0, :]).then_inc(fin_saved, 16)
                    sp.dma_start(out[(NBLOCK - 1) * P:N, :], zo[0:LASTN, 1, :]).then_inc(fin_saved, 16)
                else:
                    sp.dma_start(out[bass.ds(u * (2 * P), 2 * P), :].rearrange("(q p) c -> p q c", q=2),
                                 zo[:, :, :]).then_inc(fin_saved, 16)

            for stored in y_stored[0] + y_stored[1]:
                sp.wait_ge(stored, 16 * NPAIR * 2)
            fin_io(0, False, True)
            with sp.Fori(1, NPAIR - 1) as u:
                fin_io(u, False, False)
            fin_io(NPAIR - 1, True, False)
            sp.wait_ge(fin_saved, 16 * (NPAIR + 1))

        @blk.scalar
        def _(act):
            a_ = nc.scalar

            def take_xt(b, q, n, used):
                act.wait_ge(xt_ready, b + 1)
                if used is not None:
                    act.wait_ge(root_ready, used)
                a_.copy(h_s[:, q, 0:n], ps_xt[q][:, 0:n]).then_inc(xt_done, 1)

            def take_block(l, u, q, n, first=False):
                b = u * 2 + q
                bt = b + l * NBLOCK
                for k, (o, w) in enumerate(YCHUNK):
                    act.wait_ge(y_ready, bt * 3 + (k + 1))
                    if not first:
                        act.wait_ge(y_stored[q][k], (u + l * NPAIR) * 16)
                    a_.copy(y_out[0:n, q, o:o + w], ps_y[k][0:n, 0:w]).then_inc(y_taken, 1)
                act.wait_ge(root_ready, bt + 1)
                a_.activation(acc[:, bass.ds(b * P, n)], ps_root[:, 0:n], ACT.Identity,
                              bias=bias[l][:, 0:1]).then_inc(root_done, 1)
                if l == 1:
                    act.wait_ge(y_taken, bt * 3 + 6)
                    for k in range(len(YCHUNK)):
                        store_chunk(act, l, b, q, n, k)

            take_xt(0, 0, P, None)
            take_xt(1, 1, P, None)
            load_weights(act, 1, w_rel2, root2, b2)
            act.wait_ge(weights_in[0], 16 * 3)
            for q in range(2):
                take_block(0, 0, q, P, first=True)
                take_xt(2 + q, q, P, q + 1)
            with act.Fori(1, NPAIR - 2) as u:
                for q in range(2):
                    take_block(0, u, q, P)
                    take_xt(u * 2 + (2 + q), q, P, u * 2 + (q + 1))
            for q in range(2):
                take_block(0, NPAIR - 2, q, P)
                take_xt(NBLOCK - 2 + q, q, LASTN if q else P, NBLOCK - 3 + q)
            for q in range(2):
                take_block(0, NPAIR - 1, q, LASTN if q else P)

            act.wait_ge(weights_in[1], 16 * 3)
            act.wait_ge(typed, 2)
            stream = act.value_load(flag_i[0:1, 0:1], min_val=0, max_val=1)
            far = act.value_load(flag_i[0:1, 1:2], min_val=0, max_val=1)

            def give_indices(g, s):
                a_.copy(idx_s[:, s, :], tiles(idx_t, g)).then_inc(idx_ready, 1)

            def next_indices(l, i, s):
                act.wait_ge(agg_ready, i * U + (l * NGROUP + s + 1))
                if l == 0 and s == 0:
                    act.wait_ge(typed, i + 2)
                give_indices(i * U + (U + s), s)

            def relu(u, last=False):
                n = P + LASTN if last else 2 * P
                a_.activation(h_s[:, :, :].rearrange("p q n -> p (q n)")[:, 0:n], acc[:, bass.ds(u * (2 * P), n)],
                              ACT.Relu).then_inc(relu_done, 1)

            def pair(u, last=False):
                relu(u, last)
                for q in range(2):
                    take_block(1, u, q, LASTN if (last and q) else P)

            for s in range(U):
                give_indices(s, s)
            for start, end, behind in SPANS:
                with act.Fori(start, end) as i:
                    for s in range(U):
                        next_indices(0, i, s)
                        if behind and s in (0, 2):
                            with act.If(stream > 0):
                                if s == 0:
                                    act.wait_ge(agg_done, i * U + 1)
                                    relu(i - LAG)
                                take_block(1, i - LAG, s // 2, P)
            act.wait_ge(agg_done, NGROUP + 1)
            with act.If(far > 0):
                act.wait_ge(far_end, 1)
            with act.If(stream < 1):
                with act.Fori(0, TURNS - LAG) as u:
                    pair(u)
            pair(NPAIR - 2)
            pair(NPAIR - 1, last=True)

            def copy_pair(u, last=False):
                n = P + LASTN if last else 2 * P
                act.wait_ge(fin_ready, u + 1)
                a_.copy(h_s[:, :, :].rearrange("p q n -> p (q n)")[:, 0:n], acc[:, bass.ds(u * (2 * P), n)]
                        ).then_inc(fin_copied, 1)

            def root_of_variance(u):
                act.wait_ge(fin_z, u + 2)
                a_.activation(std[:, :], mv[:, :, 1], ACT.Sqrt, bias=eps[:, 0:1]).then_inc(fin_std, 1)

            for s in range(U):
                give_indices(s, s)
            for start, end, behind in SPANS:
                with act.Fori(start, end) as i:
                    for s in range(U):
                        next_indices(1, i, s)
                        if behind and s < 2:
                            with act.If(stream > 0):
                                if s == 0:
                                    act.wait_ge(agg_done, i * U + (NGROUP + 1))
                                    copy_pair(i - LAG)
                                else:
                                    root_of_variance(i - LAG)
            act.wait_ge(agg_done, 2 * NGROUP + 1)
            with act.If(far > 0):
                act.wait_ge(far_end, 2)
            with act.If(stream < 1):
                with act.Fori(0, TURNS - LAG) as u:
                    copy_pair(u)
                    root_of_variance(u)
            copy_pair(NPAIR - 2)
            root_of_variance(NPAIR - 2)
            copy_pair(NPAIR - 1, last=True)
            root_of_variance(NPAIR - 1)

        @blk.tensor
        def _(pe):
            t_ = nc.tensor

            def turn_x(w, r, n=P, first=False):
                w, r = w + r // XR, r % XR
                q = r % 2
                pe.wait_ge(x_loaded[r], w * 16 + 16)
                if not first:
                    pe.wait_ge(xt_done, w * XR + (r - 1))
                t_.transpose(ps_xt[q][:, 0:n], x_in[0:n, r, :], ident[0:n, 0:n]).then_inc(xt_ready, 1)

            def make_block(l, u, q, n, mid=None):
                b = u * 2 + q
                bt = b + l * NBLOCK
                h = h_s[:, q, 0:n]
                w = wall[l][:, :, :].rearrange("d r o -> d (r o)")
                for k, (o, wid) in enumerate(YCHUNK):
                    pe.wait_ge(y_taken, bt * 3 + (k + 1))
                    t_.matmul(ps_y[k][0:n, 0:wid], lhsT=h, rhs=w[:, o:o + wid], start=True, stop=True
                              ).then_inc(y_ready, 1)
                pe.wait_ge(root_done, bt + 1)
                t_.matmul(ps_root[:, 0:n], lhsT=root[l][:, :], rhs=h, start=True, stop=True
                          ).then_inc(root_ready, 1)

            pe.wait_ge(consts_done, NCONST)
            turn_x(0, 0, first=True)
            turn_x(0, 1, first=True)
            pe.wait_ge(weights_in[0], 16 * 3)

            def table_block(w, r, n=P, ahead=P):
                pe.wait_ge(xt_done, w * XR + (r + 1))
                make_block(0, w * 2 + r // 2, r % 2, n)
                if ahead:
                    turn_x(w, r + 2, ahead)

            def first_table(start, end):
                with pe.Fori(start, end) as w:
                    for r in range(XR):
                        table_block(w, r)

            first_table(0, XTURNS)
            for b in range(XTURNS * XR, NBLOCK):
                table_block(b // XR, b % XR, LASTN if b == NBLOCK - 1 else P,
                            0 if b + 2 >= NBLOCK else LASTN if b + 2 == NBLOCK - 1 else P)

            pe.wait_ge(flags_done, 1)
            stream = pe.value_load(flag_i[0:1, 0:1], min_val=0, max_val=1)
            far = pe.value_load(flag_i[0:1, 1:2], min_val=0, max_val=1)

            def count(slot):
                for j in range(GT):
                    last = t_.matmul(counts, lhsT=hit_typ[:, slot, j, :], rhs=hit[:, slot, j, :],
                                     start=(j == 0), stop=(j == GT - 1))
                return last

            with pe.If(stream < 1):
                with pe.Fori(0, NGROUP) as g:
                    pe.wait_ge(pre_hit, g + 1)
                    count(0).then_inc(pre_ready, 1)
                with pe.If(far > 0):
                    pe.wait_ge(y_taken, 3 * NBLOCK + 3)
                    with pe.Fori(0, NGROUP * GT) as t:
                        with pe.Fori(0, NFAR) as k:
                            pe.wait_ge(far_a[0], t * NFAR + k + 1)
                            t_.matmul(ps_y[0][0:R, :], lhsT=hit_typ[:, 0, 0, :], rhs=far_hitb, start=True,
                                      stop=True).then_inc(far_b[0], 1)

            def make_counts(g, s):
                pe.wait_ge(hit_ready, g + 1)
                pe.wait_ge(cnt_done, g + 1)
                count(s).then_inc(cnt_ready, 1)

            def look_up(g, s):
                base = pe.value_load(row_base[0:1, bass.ds(g, 1)], min_val=0, max_val=N - 1)
                pe.wait_ge(oh_ready, g + 1)
                pe.wait_ge(look_taken, g + 1)
                pe.wait_ge(cnt_done, g + 3)
                for j in range(GT):
                    last = t_.matmul(ps_look[:, j // 4, (j % 4) * W:(j % 4 + 1) * W],
                                     lhsT=typ_oh[:, s % 2, :].rearrange("r (p j) -> r j p", j=GT)[:, j, :],
                                     rhs=cnt[0:R, bass.ds(base, W)], start=True, stop=True)
                last.then_inc(look_ready, 1)

            pe.wait_ge(weights_in[1], 16 * 3)
            for g in range(AHEAD):
                make_counts(g, g)
            look_up(0, 0)

            def aggregate(l, i, s):
                pe.wait_ge(S_ready, i * U + (l * NGROUP + s + 1))
                pe.wait_ge(rows_in[s], i * (16 * GT) + (16 * GT * (l * TURNS + 1)))
                pe.wait_ge(agg_done, i * U + (l * NGROUP + s + 1))
                for j in range(GT):
                    last = t_.matmul(sums, lhsT=rows[:, s, j, :], rhs=S[:, s % 2, j, :],
                                     start=(j == 0), stop=(j == GT - 1))
                last.then_inc(agg_ready, 1)

            for start, end, behind in SPANS:
                with pe.Fori(start, end) as i:
                    for s in range(U):
                        g = i * U + s
                        make_counts(g + AHEAD, (s + AHEAD) % U)
                        if s < U - 1:
                            look_up(g + 1, s + 1)
                        else:
                            with pe.If(i < TURNS - 1):
                                look_up(g + 1, s + 1)
                        aggregate(0, i, s)
                        if behind and s in (0, 2):
                            with pe.If(stream > 0):
                                if s == 0:
                                    pe.wait_ge(relu_done, i - (LAG - 1))
                                make_block(1, i - LAG, s // 2, P)
            with pe.If(far > 0):
                with pe.Fori(0, NGROUP) as g:
                    for j in range(GT):
                        with pe.Fori(0, NFAR) as k:
                            pe.wait_ge(far_a[1], g * (GT * NFAR) + (k + (j * NFAR + 1)))
                            t_.matmul(ps_y[0][:, :], lhsT=typ_oh[:, 0, :].rearrange("r (p j) -> r j p", j=GT)[:, j, :],
                                      rhs=cnt[0:R, bass.ds(k * FARW, FARW)], start=True, stop=True
                                      ).then_inc(far_b[1], 1)

            def far_sums(l):
                with pe.Fori(0, NGROUP * GT) as t:
                    with pe.Fori(0, NFAR) as k:
                        pe.wait_ge(far_rows[l], t * 16 + 16)
                        pe.wait_ge(far_a[2 + l], t * NFAR + k + 1)
                        t_.matmul(ps_y[0][:, :], lhsT=rows[:, 0, 0, :], rhs=far_hit, start=True,
                                  stop=True).then_inc(far_b[2 + l], 1)

            with pe.If(far > 0):
                far_sums(0)
            with pe.If(stream < 1):
                with pe.Fori(0, TURNS - LAG) as u:
                    pe.wait_ge(relu_done, u + 1)
                    for q in range(2):
                        make_block(1, u, q, P)
            for u in (NPAIR - 2, NPAIR - 1):
                pe.wait_ge(relu_done, u + 1)
                for q in range(2):
                    make_block(1, u, q, LASTN if (u == NPAIR - 1 and q) else P)

            def turn_pair(u, last=False):
                pe.wait_ge(fin_z, u + 1)
                pe.wait_ge(fin_copied, u + 1)
                for q in range(2):
                    n = LASTN if (last and q) else P
                    ins = t_.transpose(ps_fin[0:n, q, :], h_s[:, q, 0:n], ident[:, :])
                ins.then_inc(fin_ready, 1)

            for start, end, behind in SPANS:
                with pe.Fori(start, end) as i:
                    for s in range(U):
                        aggregate(1, i, s)
                        if behind and s == 0:
                            with pe.If(stream > 0):
                                turn_pair(i - LAG)
            with pe.If(far > 0):
                pe.wait_ge(y_taken, 6 * NBLOCK + 3)
                far_sums(1)
            with pe.If(stream < 1):
                with pe.Fori(0, TURNS - LAG) as u:
                    turn_pair(u)
            turn_pair(NPAIR - 2)
            turn_pair(NPAIR - 1, last=True)

        @blk.vector
        def _(dve):
            v_ = nc.vector
            steps = [0]

            def link(ins):
                steps[0] += 1
                ins.then_inc(own, 1)
                dve.wait_ge(own, steps[0])

            def link_in(k, i, per, n, ins):
                ins.then_inc(own_loop[k], 1)
                dve.wait_ge(own_loop[k], i * per + (n + 1))

            dve.sem_inc(y_taken, 3)
            dve.sem_inc(root_done, 1)
            dve.sem_inc(look_taken, 1)
            dve.sem_inc(agg_done, 1)
            dve.sem_inc(pre_typed, 1)
            for credited in (pre_done, cnt_done, fin_ready, fin_z, fin_out, *far_v):
                dve.sem_inc(credited, 1)

            v_.memset(dst_i[1][64:HALF[1][1], :], int(PADDST)).then_inc(pad_set, 1)
            v_.memset(dst_e[:, (NGROUP - 1) * GT:NG * GT], int(PADDST)).then_inc(pad_set, 1)
            v_.memset(idx_t[:, (NGROUP - 1) * GT:NG * GT], 0).then_inc(pad_set, 1)
            v_.memset(acc[:, N:NCOL], 0.0).then_inc(pad_set, 1)
            link(v_.memset(row_min[:, :], float(N)))
            link(v_.memset(row_max[:, :], float(N)))
            link(v_.memset(rel_t[:, NGROUP * GT:NG * GT], PADDST))
            link(v_.memset(typ_t[:, NGROUP * GT:NG * GT], 0.0))
            dve.wait_ge(consts_done, NCONST)

            dve.wait_ge(groups_in, 16 * 4)
            for h, (g0, ng) in enumerate(HALF):
                link(v_.tensor_copy(dst_f[h][0:ng, :], dst_i[h][0:ng, :]))
                link(v_.tensor_reduce(out=gmin[0:ng, h:h + 1], in_=dst_f[h][0:ng, :], op=ALU.min, axis=AX.X))
                link(v_.scalar_tensor_tensor(out=dst_m[h][0:ng, :], in0=dst_f[h][0:ng, :], scalar=PADDST / 2,
                                             in1=dst_f[h][0:ng, :], op0=ALU.is_lt, op1=ALU.mult))
                v_.tensor_reduce(out=gmax[0:ng, h:h + 1], in_=dst_m[h][0:ng, :], op=ALU.max, axis=AX.X
                                 ).then_inc(grouped, 1)
            NT = NGROUP * GT
            dve.wait_ge(edges_in, 16 * 4)
            link(v_.tensor_copy(rel_t[:, 0:NT], dst_e[:, 0:NT]))
            link(v_.tensor_scalar(far_t[:, 0:NT], rel_t[:, 0:NT], 1.0, None, ALU.add))
            dve.wait_ge(minmax_in, 48)
            grouped_rel = rel_t[:, 0:NT].rearrange("p (g j) -> p g j", j=GT)
            link(v_.tensor_tensor(grouped_rel, grouped_rel, base_all[:, :].rearrange("p (g u) -> p g u", u=1)
                                  .to_broadcast([P, NGROUP, GT]), ALU.subtract))
            link(v_.scalar_tensor_tensor(out=far_t[:, 0:NT], in0=rel_t[:, 0:NT], scalar=float(W),
                                         in1=far_t[:, 0:NT], op0=ALU.is_ge, op1=ALU.mult))
            link(v_.tensor_scalar(far_t[:, 0:NT], far_t[:, 0:NT], -1.0, None, ALU.add))
            link(v_.memset(cnt[:, :], 0.0))
            G_ = NGROUP
            link(v_.tensor_copy(row_base[:, :], row_min[:, :]))
            link(v_.tensor_tensor(row_tmp[:, 0:G_], row_max[:, 0:G_], row_min[:, 0:G_], ALU.subtract))
            link(v_.tensor_reduce(out=flag[:, 0:1], in_=row_tmp[:, 0:G_], op=ALU.max, axis=AX.X))
            link(v_.tensor_scalar(flag[:, 1:2], flag[:, 0:1], float(W), None, ALU.is_ge))
            link(v_.tensor_tensor(row_tmp[:, 0:G_ - 1], row_min[:, 1:G_], row_max[:, 0:G_ - 1], ALU.is_ge))
            link(v_.tensor_reduce(out=flag[:, 2:3], in_=row_tmp[:, 0:G_ - 1], op=ALU.min, axis=AX.X))
            link(v_.tensor_tensor(row_tmp[:, 0:G_ - 2], row_min[:, 2:G_], row_min[:, 0:G_ - 2], ALU.subtract))
            link(v_.tensor_scalar(row_tmp[:, 0:G_ - 2], row_tmp[:, 0:G_ - 2], float(W), None, ALU.is_ge))
            link(v_.tensor_reduce(out=flag[:, 3:4], in_=row_tmp[:, 0:G_ - 2], op=ALU.min, axis=AX.X))
            first = row_min[:, 0:G_].rearrange("a (i u) -> a i u", u=U)[:, :, 0]
            link(v_.tensor_tensor(row_tmp[:, LAG:TURNS], first[:, LAG:TURNS], turn_min[:, LAG:TURNS], ALU.is_ge))
            link(v_.tensor_reduce(out=flag[:, 4:5], in_=row_tmp[:, LAG:TURNS], op=ALU.min, axis=AX.X))
            link(v_.tensor_scalar(flag[:, 5:6], flag[:, 1:2], 1.0, None, ALU.is_lt))
            link(v_.tensor_reduce(out=flag[:, 6:7], in_=flag[:, 2:6], op=ALU.min, axis=AX.X))
            link(v_.tensor_scalar(row_tmp[:, :], row_min[:, :], -float(SPARE), None, ALU.add))
            link(v_.tensor_scalar(row_tmp[:, :], row_tmp[:, :], flag[:, 6:7], float(SPARE), ALU.mult, ALU.add))
            link(v_.memset(row_tmp[:, G_:NG], float(SPARE)))
            link(v_.tensor_copy(row_count[:, :], row_tmp[:, :]))
            link(v_.tensor_copy(flag_i[:, 0:1], flag[:, 6:7]))
            link(v_.tensor_copy(flag_i[:, 1:2], flag[:, 1:2]))
            dve.sem_inc(flags_done, 1)
            stream = dve.value_load(flag_i[0:1, 0:1], min_val=0, max_val=1)
            far = dve.value_load(flag_i[0:1, 1:2], min_val=0, max_val=1)

            def bc(ap, n, w):
                return ap.rearrange("p (n u) -> p n u", u=1).to_broadcast([P, n, w])

            def bc1(ap, n, w):
                return ap.rearrange("p (u w) -> p u w", u=1).to_broadcast([P, n, w])

            def make_hit(slot, g):
                return v_.tensor_tensor(hit[:, slot, :, :], bc1(iota_w[:, :], GT, W), bc(tiles(rel_t, g), GT, W),
                                        ALU.is_equal)

            def make_hit_typ(slot, g):
                return v_.tensor_tensor(hit_typ[:, slot, :, :], bc1(iota_r[:, :], GT, R), bc(tiles(typ_t, g), GT, R),
                                        ALU.is_equal)

            def count_window(row, g):
                return cnt[0:R, bass.ds(dve.value_load(row[0:1, bass.ds(g, 1)], min_val=0, max_val=SPARE), W)]

            def make_types(turn, chain, before, used, again=False):
                cols = bass.ds(turn * (U * GT), U * GT)

                def step(n, ins):
                    ins.then_inc(chain, 1)
                    dve.wait_ge(chain, before + (n + 1))

                a = attr[:, :, TYPE0:TYPE0 + R]
                step(0, v_.tensor_reduce(out=amax[:, :], in_=a, op=ALU.max, axis=AX.X))
                step(1, v_.tensor_tensor(ahit[:, :, :], a, bc(amax[:, :], U * GT, R), ALU.is_equal))
                dve.sem_inc(used, 1)
                step(2, v_.tensor_tensor(ahit[:, :, :], ahit[:, :, :], bc1(rev_r[:, :], U * GT, R), ALU.mult))
                step(3, v_.tensor_reduce(out=typ_t[:, cols], in_=ahit[:, :, :], op=ALU.max, axis=AX.X))
                step(4, v_.tensor_scalar(typ_t[:, cols], typ_t[:, cols], -1.0, float(R), ALU.mult, ALU.add))
                if not again:
                    v_.scalar_tensor_tensor(out=idx_t[:, cols], in0=idx_t[:, cols], scalar=float(R),
                                            in1=typ_t[:, cols], op0=ALU.mult, op1=ALU.add).then_inc(typed, 1)
                    dve.wait_ge(typed, turn + 1)
                dve.sem_inc(held, 1)

            def far_windows(t):
                return v_.tensor_scalar(far_d[:, :], far0[:, :], -1.0, far_t[:, bass.ds(t, 1)], ALU.mult, ALU.add)

            with dve.If(stream < 1):
                with dve.Fori(0, TURNS - 1) as i:
                    dve.wait_ge(pre_attr, i * 16 + 16)
                    make_types(i, own_loop[1], i * 5, pre_typed, again=True)
                dve.wait_ge(pre_attr, (TURNS + 1) * 16)
                make_types(TURNS - 1, own_loop[1], (TURNS - 1) * 5, pre_typed, again=True)
                with dve.Fori(0, NGROUP) as g:
                    make_hit(0, g)
                    make_hit_typ(0, g).then_inc(pre_hit, 1)
                    win = count_window(row_base, g)
                    dve.wait_ge(pre_done, g + 1)
                    dve.wait_ge(pre_ready, g + 1)
                    v_.tensor_tensor(win, counts, win, ALU.add).then_inc(pre_done, 1)
                with dve.If(far > 0):
                    with dve.Fori(0, NT) as t:
                        dve.wait_ge(far_v[0], t * (NFAR + 1) + 1)
                        v_.tensor_scalar(hit_typ[:, 0, 0, :], iota_r[:, :], typ_t[:, bass.ds(t, 1)], None,
                                         ALU.is_equal)
                        far_windows(t).then_inc(far_v[0], 1)
                        with dve.Fori(0, NFAR) as k:
                            dve.wait_ge(far_v[0], t * (NFAR + 1) + k + 2)
                            v_.tensor_scalar(far_hitb, iota_far[:, :], far_d[:, bass.ds(k, 1)], None,
                                             ALU.is_equal).then_inc(far_a[0], 1)
                            dve.wait_ge(far_b[0], t * NFAR + k + 1)
                            win = cnt[0:R, bass.ds(k * FARW, FARW)]
                            v_.tensor_tensor(win, ps_y[0][0:R, :], win, ALU.add).then_inc(far_v[0], 1)

            for i in range(2):
                dve.wait_ge(first_attr, i * 16 + 16)
                make_types(i, own_loop[0], i * 5, attr_used)
            for g in range(U):
                make_hit(g, g)
                make_hit_typ(g, g).then_inc(hit_ready, 1)

            def add_counts(g):
                win = count_window(row_count, g)
                dve.wait_ge(cnt_ready, g + 1)
                dve.wait_ge(cnt_done, g + 1)
                v_.tensor_tensor(win, counts, win, ALU.add).then_inc(cnt_done, 1)

            for g in range(AHEAD):
                add_counts(g)

            def type_onehot(q, full):
                dve.wait_ge(typ_in[q], full)
                v_.tensor_scalar(typ_oh[:, q, :], typ_oh[:, q, :], part[0:R, 0:1], None, ALU.is_equal
                                 ).then_inc(oh_ready, 1)

            def make_S(i, s):
                return v_.tensor_tensor(S[:, s % 2, :, :], hit[:, s, :, :], bc(tiles(c_t, i * U + s), GT, W),
                                        ALU.mult)

            def add_sums(l, i, s):
                g = i * U + s
                base = dve.value_load(row_base[0:1, bass.ds(g, 1)], min_val=0, max_val=N - 1)
                dve.wait_ge(agg_ready, g + (l * NGROUP + 1))
                dve.wait_ge(agg_done, g + (l * NGROUP + 1))
                win = acc[:, bass.ds(base, W)]
                v_.tensor_tensor(win, sums, win, ALU.add).then_inc(agg_done, 1)

            type_onehot(0, 16)
            type_onehot(1, 16)
            dve.wait_ge(root_done, NBLOCK + 1)
            with dve.Fori(0, TURNS) as i:
                for s in range(U):
                    g = i * U + s
                    dve.wait_ge(look_ready, g + 1)
                    m = hit[:, s, :, :].rearrange("p (a b) w -> p a (b w)", a=2)
                    ins = v_.tensor_tensor(looked[:, :, :].rearrange("p (a b) w -> p a (b w)", a=2), m,
                                           ps_look[:, :, 0:4 * W], ALU.mult)
                    ins.then_inc(look_taken, 1)
                    dve.wait_ge(look_taken, g + 2)
                    link_in(2, i, 3 * U, 3 * s, v_.tensor_reduce(out=cnt_e[:, :], in_=looked[:, :, :], op=ALU.add,
                                                                 axis=AX.X))
                    link_in(2, i, 3 * U, 3 * s + 1, v_.tensor_scalar(cnt_e[:, :], cnt_e[:, :], 1.0, None, ALU.max))
                    link_in(2, i, 3 * U, 3 * s + 2, v_.reciprocal(tiles(c_t, g), cnt_e[:, :]))
                    make_S(i, s).then_inc(S_ready, 1)
                    if s < U - 2:
                        type_onehot(s % 2, i * 32 + (16 * (s // 2) + 32))
                    else:
                        with dve.If(i < TURNS - 1):
                            type_onehot(s % 2, i * 32 + (16 * (s // 2) + 32))
                    if s:
                        add_sums(0, i, s - 1)
                    dve.wait_ge(S_ready, g + 1)
                    make_hit(s, g + U)
                    make_hit_typ(s, g + U).then_inc(hit_ready, 1)
                    add_counts(g + AHEAD)
                    if s == 1:
                        with dve.If(i < TURNS - 3):
                            dve.wait_ge(attr_in, i * 16 + 16)
                            make_types(i + 2, own_loop[0], i * 5 + 10, attr_used)
                        with dve.If(i > TURNS - 4):
                            with dve.If(i < TURNS - 2):
                                dve.wait_ge(attr_in, (TURNS - 1) * 16)
                                make_types(TURNS - 1, own_loop[0], (TURNS - 1) * 5, attr_used)
                            with dve.If(i > TURNS - 3):
                                dve.sem_inc(typed, 1)
                add_sums(0, i, U - 1)

            def far_sums(l):
                v = far_v[2 + l]
                dve.wait_ge(idx_ready, (l + 1) * (NGROUP + U))
                with dve.Fori(0, NT) as t:
                    dve.wait_ge(v, t * (NFAR + 1) + 1)
                    v_.tensor_copy(idx_s[:, 0, 0:1], idx_t[:, bass.ds(t, 1)]).then_inc(far_idx[l], 1)
                    far_windows(t).then_inc(v, 1)
                    with dve.Fori(0, NFAR) as k:
                        dve.wait_ge(v, t * (NFAR + 1) + k + 2)
                        v_.tensor_scalar(far_hit, iota_far[:, :], far_d[:, bass.ds(k, 1)],
                                         c_t[:, bass.ds(t, 1)], ALU.is_equal, ALU.mult).then_inc(far_a[2 + l], 1)
                        dve.wait_ge(far_b[2 + l], t * NFAR + k + 1)
                        win = acc[:, bass.ds(k * FARW, FARW)]
                        v_.tensor_tensor(win, ps_y[0][:, :], win, ALU.add).then_inc(v, 1)
                dve.wait_ge(v, NT * (NFAR + 1) + 1)

            FARSTEPS = 1 + GT * (NFAR + 5)
            dve.wait_ge(agg_done, NGROUP + 1)
            with dve.If(far > 0):
                with dve.Fori(0, NGROUP) as g:
                    dve.wait_ge(far_v[1], g * FARSTEPS + 1)
                    dve.sem_inc(far_ask, 1)
                    dve.wait_ge(far_typ, g * 16 + 16)
                    v_.tensor_scalar(typ_oh[:, 0, :], typ_oh[:, 0, :], part[0:R, 0:1], None, ALU.is_equal
                                     ).then_inc(far_v[1], 1)
                    for j in range(GT):
                        t = g * GT + j
                        done = g * FARSTEPS + (j * (NFAR + 5) + 2)
                        dve.wait_ge(far_v[1], done)
                        far_windows(t).then_inc(far_v[1], 1)
                        with dve.Fori(0, NFAR) as k:
                            dve.wait_ge(far_v[1], done + k + 1)
                            dve.sem_inc(far_a[1], 1)
                            dve.wait_ge(far_b[1], t * NFAR + k + 1)
                            v_.scalar_tensor_tensor(out=far_hit, in0=iota_far[:, :], scalar=far_d[:, bass.ds(k, 1)],
                                                    in1=ps_y[0][:, :], op0=ALU.is_equal, op1=ALU.mult,
                                                    accum_out=far_c[:, bass.ds(k, 1)]).then_inc(far_v[1], 1)
                        dve.wait_ge(far_v[1], done + (NFAR + 1))
                        v_.tensor_reduce(out=cnt_e[:, 0:1], in_=far_c[:, :], op=ALU.add, axis=AX.X
                                         ).then_inc(far_v[1], 1)
                        dve.wait_ge(far_v[1], done + (NFAR + 2))
                        v_.tensor_scalar(cnt_e[:, 0:1], cnt_e[:, 0:1], 1.0, None, ALU.max).then_inc(far_v[1], 1)
                        dve.wait_ge(far_v[1], done + (NFAR + 3))
                        v_.reciprocal(cnt_e[:, 1:2], cnt_e[:, 0:1]).then_inc(far_v[1], 1)
                        dve.wait_ge(far_v[1], done + (NFAR + 4))
                        cc = c_t[:, bass.ds(t, 1)]
                        v_.tensor_tensor(cc, cc, cnt_e[:, 1:2], ALU.mult).then_inc(far_v[1], 1)
                dve.wait_ge(far_v[1], NGROUP * FARSTEPS + 1)
                far_sums(0)
                dve.sem_inc(far_end, 1)

            dve.wait_ge(root_done, 2 * NBLOCK + 1)

            def residual(u, last=False):
                dve.wait_ge(fin_out, u + 1)
                dve.wait_ge(fin_ready, u + 2)
                dve.wait_ge(fin_x, u * 16 + (32 if last else 16))
                if last:
                    v_.tensor_tensor(z[:, 0, :], ps_fin[:, 0, :], x_in[:, 0, :], ALU.add)
                    v_.tensor_tensor(z[0:LASTN, 1, :], ps_fin[0:LASTN, 1, :], x_in[0:LASTN, 1, :], ALU.add
                                     ).then_inc(own_loop[4], 1)
                else:
                    v_.tensor_tensor(z, ps_fin, x_in[:, 0:2, :], ALU.add).then_inc(own_loop[4], 1)
                dve.wait_ge(own_loop[4], u + 1)
                for q in range(2):
                    v_.bn_stats(stats[:, q, :], z[:, q, :]).then_inc(own_loop[5], 1)
                dve.wait_ge(own_loop[5], u * 2 + 2)
                dve.sem_inc(held, 1)
                v_.bn_aggr(mv[:, 0, :], stats[:, 0, :])
                v_.bn_aggr(mv[:, 1, :], stats[:, 1, :]).then_inc(fin_z, 1)

            def normalise(u):
                dve.wait_ge(fin_std, u + 1)
                v_.reciprocal(rstd[:, :], std[:, :]).then_inc(own_loop[6], 1)
                dve.wait_ge(own_loop[6], u + 1)
                for q in range(2):
                    ins = v_.tensor_scalar(zo[:, q, :], z[:, q, :], mv[:, q, 0:1], rstd[:, q:q + 1],
                                           ALU.subtract, ALU.mult)
                ins.then_inc(fin_out, 1)

            for start, end, behind in SPANS:
                with dve.Fori(start, end) as i:
                    for s in range(U):
                        g = i * U + s
                        dve.wait_ge(S_ready, g + (NGROUP - U + 1))
                        link_in(7, i, U, s, make_hit(s, g))
                        make_S(i, s).then_inc(S_ready, 1)
                        if s >= 1:
                            add_sums(1, i, s - 1)
                        if behind and s in (1, 2):
                            with dve.If(stream > 0):
                                if s == 1:
                                    residual(i - LAG)
                                else:
                                    normalise(i - LAG)
                    add_sums(1, i, U - 1)
            dve.wait_ge(agg_done, 2 * NGROUP + 1)
            with dve.If(far > 0):
                far_sums(1)
                dve.sem_inc(far_end, 1)
            with dve.If(stream < 1):
                with dve.Fori(0, TURNS - LAG) as u:
                    residual(u)
                    normalise(u)
            residual(NPAIR - 2)
            normalise(NPAIR - 2)
            residual(NPAIR - 1, last=True)
            normalise(NPAIR - 1)


_INS = ['x', 'src', 'dst', 'edge_attr_42', 'L0_gnn_w_rel1', 'L0_gnn_root1', 'L0_gnn_b1',
        'L0_gnn_w_rel2', 'L0_gnn_root2', 'L0_gnn_b2']


def kernel(**inputs):
    import numpy as _np
    import concourse.bacc as _bacc
    from concourse import mybir as _mybir
    from concourse.bass_utils import run_bass_kernel_spmd as _run

    nc = _bacc.Bacc("TRN2", target_bir_lowering=False, num_devices=1)
    arrays, args = {}, []
    for name in _INS:
        a = _np.ascontiguousarray(inputs[name])
        arrays[f"in_{name}_dram"] = a
        args.append(nc.dram_tensor(f"in_{name}_dram", a.shape, _mybir.dt.from_np(a.dtype), kind="ExternalInput").ap())
    out = nc.dram_tensor("out_0_dram", (N, C), F32, kind="ExternalOutput").ap()
    table1 = nc.dram_tensor("table1", (N * R, C), F32, kind="Internal").ap()
    table2 = nc.dram_tensor("table2", (N * R, C), F32, kind="Internal").ap()
    type_row = nc.dram_tensor("type_row", (NGROUP, GE), F32, kind="Internal").ap()
    row_scratch = nc.dram_tensor("row_scratch", (2, NGROUP), F32, kind="Internal").ap()
    gnn_kernel(nc, *args, out, table1, table2, type_row, row_scratch)
    r = _run(nc, [arrays], core_ids=[0])
    return r.results[0]["out_0_dram"]
```
